# Optimizing a Trainium2 kernel written in Bass

```python
import numpy as np
import jax
import jax.numpy as jnp

def _softmax(x, axis=-1):
    return jax.nn.softmax(x, axis=axis)

def _gelu(x):
    return jax.nn.gelu(x, approximate=True)

def _silu(x):
    return jax.nn.silu(x)

def _sigmoid(x):
    return jax.nn.sigmoid(x)

def _layernorm(x, axis=-1, eps=1e-05):
    m = jnp.mean(x, axis=axis, keepdims=True)
    v = jnp.var(x, axis=axis, keepdims=True)
    return (x - m) / jnp.sqrt(v + eps)

def _scatter_add(tgt, idx, src, axis=0):
    return tgt.at[idx].add(src)

def _segment_sum(src, seg, n):
    return jax.ops.segment_sum(src, seg, n)
kernel_name = 'mk_recurrent_d1_jaxref_r4_c70a21'

def setup_inputs(seed: int=0):
    np.random.seed(seed)
    _w = jnp.asarray

    def _L0_attn_setup():
        import jax, jax.numpy as jnp
        import numpy as np
        B, S, D, H = (4, 512, 256, 16)
        DK = D // H
        key = jax.random.key(seed)
        kx, kq, kk, kv, ko = jax.random.split(key, 5)
        scale = D ** (-0.5)
        return {'x': jax.random.normal(kx, (B, S, D), dtype=jnp.float32), 'W_q': jax.random.normal(kq, (D, D), dtype=jnp.float32) * scale, 'W_k': jax.random.normal(kk, (D, D), dtype=jnp.float32) * scale, 'W_v': jax.random.normal(kv, (D, D), dtype=jnp.float32) * scale, 'W_o': jax.random.normal(ko, (D, D), dtype=jnp.float32) * scale}
    _L0_attn_in = _L0_attn_setup()

    def _L0_ffn_setup():
        import jax, jax.numpy as jnp
        import numpy as np
        DIM = 256
        DEPTH = 2
        HEADS = 8
        DIM_HEAD = 64
        WINDOW = 128
        INNER = HEADS * DIM_HEAD
        HID = int(DIM * 4 * 2 / 3)
        B, N = (2, 2048)
        QK_SCALE = 8.0

        def shift_token(t):
            t1, t2 = jnp.split(t, 2, axis=-1)
            t2 = jnp.pad(t2, ((0, 0), (1, 0), (0, 0)))[:, :-1]
            return jnp.concatenate([t1, t2], axis=-1)

        def l2norm(t):
            return t / jnp.clip(jnp.linalg.norm(t, axis=-1, keepdims=True), 1e-12)

        def rotate_half(x):
            x1, x2 = jnp.split(x, 2, axis=-1)
            return jnp.concatenate([-x2, x1], axis=-1)

        def rotary_xpos(q, k):
            n = q.shape[-2]
            half_idx = jnp.arange(0, DIM_HEAD, 2, dtype=jnp.float32)
            inv_freq = 1.0 / 10000.0 ** (half_idx / DIM_HEAD)
            t = jnp.arange(n, dtype=jnp.float32)
            freqs = t[:, None] * inv_freq[None, :]
            freqs = jnp.concatenate([freqs, freqs], axis=-1)
            base = (half_idx + 0.4 * DIM_HEAD) / (1.4 * DIM_HEAD)
            power = (t - n // 2) / float(WINDOW // 2)
            scale = base[None, :] ** power[:, None]
            scale = jnp.concatenate([scale, scale], axis=-1)
            cos, sin = (jnp.cos(freqs), jnp.sin(freqs))
            q = q * cos * scale + rotate_half(q) * sin * scale
            k = k * cos / scale + rotate_half(k) * sin / scale
            return (q, k)

        def local_attention(q, k, v):
            b, h, n, d = q.shape
            w = n // WINDOW
            bq = q.reshape(b, h, w, WINDOW, d) * QK_SCALE
            bk = k.reshape(b, h, w, WINDOW, d)
            bv = v.reshape(b, h, w, WINDOW, d)

            def look_around(t):
                p = jnp.pad(t, ((0, 0), (0, 0), (1, 0), (0, 0), (0, 0)))
                return jnp.concatenate([p[:, :, :w], p[:, :, 1:]], axis=3)
            bk, bv = (look_around(bk), look_around(bv))
            bt = jnp.arange(n).reshape(w, WINDOW)
            btp = jnp.pad(bt, ((1, 0), (0, 0)), constant_values=-1)
            btk = jnp.concatenate([btp[:w], btp[1:]], axis=1)
            sim = jnp.einsum('bhwid,bhwjd->bhwij', bq, bk)
            i = bt[:, :, None]
            j = btk[:, None, :]
            mask = (i < j) | (i > j + WINDOW) | (j == -1)
            sim = jnp.where(mask, -jnp.finfo(sim.dtype).max, sim)
            attn = jax.nn.softmax(sim, axis=-1)
            out = jnp.einsum('bhwij,bhwjd->bhwid', attn, bv)
            return out.reshape(b, h, n, d)

        def _layer(x, wqkv, qs, ksc, wo, lg, lb, w1, b1, w2, b2):
            b, n, _ = x.shape
            h = shift_token(x)
            qkv = h @ wqkv
            q, k, v = jnp.split(qkv, 3, axis=-1)
            to_heads = lambda t: t.reshape(b, n, HEADS, DIM_HEAD).transpose(0, 2, 1, 3)
            q, k, v = (to_heads(q), to_heads(k), to_heads(v))
            q = l2norm(q) * qs
            k = l2norm(k) * ksc
            q, k = rotary_xpos(q, k)
            o = local_attention(q, k, v)
            o = o.transpose(0, 2, 1, 3).reshape(b, n, INNER)
            x = x + o @ wo
            h = shift_token(x)
            mu = h.mean(-1, keepdims=True)
            var = h.var(-1, keepdims=True)
            h = (h - mu) / jnp.sqrt(var + 1e-05) * lg + lb
            h = h @ w1 + b1
            a, g = jnp.split(h, 2, axis=-1)
            h = a * jax.nn.gelu(g, approximate=False)
            x = x + h @ w2 + b2
            return x
        key = jax.random.key(seed)
        ks = jax.random.split(key, 6)
        return {'x': jax.random.normal(ks[0], (B, N, DIM), jnp.float32), 'wqkv': jax.random.normal(ks[1], (DEPTH, DIM, 3 * INNER), jnp.float32) * 0.02, 'q_scale': jnp.ones((DEPTH, DIM_HEAD), jnp.float32), 'k_scale': jnp.ones((DEPTH, DIM_HEAD), jnp.float32), 'wo': jax.random.normal(ks[2], (DEPTH, INNER, DIM), jnp.float32) * 0.02, 'ln_g': jnp.ones((DEPTH, DIM), jnp.float32), 'ln_b': jnp.zeros((DEPTH, DIM), jnp.float32), 'w1': jax.random.normal(ks[3], (DEPTH, DIM, 2 * HID), jnp.float32) * 0.02, 'b1': jnp.zeros((DEPTH, 2 * HID), jnp.float32), 'w2': jax.random.normal(ks[4], (DEPTH, HID, DIM), jnp.float32) * 0.02, 'b2': jnp.zeros((DEPTH, DIM), jnp.float32)}
    _L0_ffn_in = _L0_ffn_setup()
    _d = {'L0_attn_x': _L0_attn_in['x'], 'L0_attn_W_q': _L0_attn_in['W_q'], 'L0_attn_W_k': _L0_attn_in['W_k'], 'L0_attn_W_v': _L0_attn_in['W_v'], 'L0_attn_W_o': _L0_attn_in['W_o'], 'L0_ffn_wqkv': _L0_ffn_in['wqkv'], 'L0_ffn_q_scale': _L0_ffn_in['q_scale'], 'L0_ffn_k_scale': _L0_ffn_in['k_scale'], 'L0_ffn_wo': _L0_ffn_in['wo'], 'L0_ffn_ln_g': _L0_ffn_in['ln_g'], 'L0_ffn_ln_b': _L0_ffn_in['ln_b'], 'L0_ffn_w1': _L0_ffn_in['w1'], 'L0_ffn_b1': _L0_ffn_in['b1'], 'L0_ffn_w2': _L0_ffn_in['w2'], 'L0_ffn_b2': _L0_ffn_in['b2']}
    _x0 = _d['L0_attn_x']
    _d['L0_attn_x'] = jax.random.normal(jax.random.fold_in(jax.random.key(seed), 1), (4, 1024, 256), dtype=_x0.dtype)
    del _x0
    return _d

def reference(L0_attn_x, L0_attn_W_q, L0_attn_W_k, L0_attn_W_v, L0_attn_W_o, L0_ffn_wqkv, L0_ffn_q_scale, L0_ffn_k_scale, L0_ffn_wo, L0_ffn_ln_g, L0_ffn_ln_b, L0_ffn_w1, L0_ffn_b1, L0_ffn_w2, L0_ffn_b2):

    def _L0_attn_ref(x, W_q, W_k, W_v, W_o):
        import jax, jax.numpy as jnp
        import numpy as np
        B, S, D, H = (4, 512, 256, 16)
        DK = D // H
        b, s, d = x.shape

        def proj(W):
            return (x @ W.T).reshape(b, s, H, DK).transpose(0, 2, 1, 3)
        Q, K, V = (proj(W_q), proj(W_k), proj(W_v))
        scores = jnp.einsum('bhqd,bhkd->bhqk', Q, K) * DK ** (-0.5)
        causal = jnp.tril(jnp.ones((s, s), dtype=bool))
        scores = jnp.where(causal, scores, -jnp.inf)
        attn = jax.nn.softmax(scores, axis=-1)
        out = jnp.einsum('bhqk,bhkd->bhqd', attn, V)
        out = out.transpose(0, 2, 1, 3).reshape(b, s, d)
        return out @ W_o.T

    def _L0_ffn_ref(x, wqkv, q_scale, k_scale, wo, ln_g, ln_b, w1, b1, w2, b2):
        import jax, jax.numpy as jnp
        import numpy as np
        DIM = 256
        DEPTH = 2
        HEADS = 8
        DIM_HEAD = 64
        WINDOW = 128
        INNER = HEADS * DIM_HEAD
        HID = int(DIM * 4 * 2 / 3)
        B, N = (2, 2048)
        QK_SCALE = 8.0

        def shift_token(t):
            t1, t2 = jnp.split(t, 2, axis=-1)
            t2 = jnp.pad(t2, ((0, 0), (1, 0), (0, 0)))[:, :-1]
            return jnp.concatenate([t1, t2], axis=-1)

        def l2norm(t):
            return t / jnp.clip(jnp.linalg.norm(t, axis=-1, keepdims=True), 1e-12)

        def rotate_half(x):
            x1, x2 = jnp.split(x, 2, axis=-1)
            return jnp.concatenate([-x2, x1], axis=-1)

        def rotary_xpos(q, k):
            n = q.shape[-2]
            half_idx = jnp.arange(0, DIM_HEAD, 2, dtype=jnp.float32)
            inv_freq = 1.0 / 10000.0 ** (half_idx / DIM_HEAD)
            t = jnp.arange(n, dtype=jnp.float32)
            freqs = t[:, None] * inv_freq[None, :]
            freqs = jnp.concatenate([freqs, freqs], axis=-1)
            base = (half_idx + 0.4 * DIM_HEAD) / (1.4 * DIM_HEAD)
            power = (t - n // 2) / float(WINDOW // 2)
            scale = base[None, :] ** power[:, None]
            scale = jnp.concatenate([scale, scale], axis=-1)
            cos, sin = (jnp.cos(freqs), jnp.sin(freqs))
            q = q * cos * scale + rotate_half(q) * sin * scale
            k = k * cos / scale + rotate_half(k) * sin / scale
            return (q, k)

        def local_attention(q, k, v):
            b, h, n, d = q.shape
            w = n // WINDOW
            bq = q.reshape(b, h, w, WINDOW, d) * QK_SCALE
            bk = k.reshape(b, h, w, WINDOW, d)
            bv = v.reshape(b, h, w, WINDOW, d)

            def look_around(t):
                p = jnp.pad(t, ((0, 0), (0, 0), (1, 0), (0, 0), (0, 0)))
                return jnp.concatenate([p[:, :, :w], p[:, :, 1:]], axis=3)
            bk, bv = (look_around(bk), look_around(bv))
            bt = jnp.arange(n).reshape(w, WINDOW)
            btp = jnp.pad(bt, ((1, 0), (0, 0)), constant_values=-1)
            btk = jnp.concatenate([btp[:w], btp[1:]], axis=1)
            sim = jnp.einsum('bhwid,bhwjd->bhwij', bq, bk)
            i = bt[:, :, None]
            j = btk[:, None, :]
            mask = (i < j) | (i > j + WINDOW) | (j == -1)
            sim = jnp.where(mask, -jnp.finfo(sim.dtype).max, sim)
            attn = jax.nn.softmax(sim, axis=-1)
            out = jnp.einsum('bhwij,bhwjd->bhwid', attn, bv)
            return out.reshape(b, h, n, d)

        def _layer(x, wqkv, qs, ksc, wo, lg, lb, w1, b1, w2, b2):
            b, n, _ = x.shape
            h = shift_token(x)
            qkv = h @ wqkv
            q, k, v = jnp.split(qkv, 3, axis=-1)
            to_heads = lambda t: t.reshape(b, n, HEADS, DIM_HEAD).transpose(0, 2, 1, 3)
            q, k, v = (to_heads(q), to_heads(k), to_heads(v))
            q = l2norm(q) * qs
            k = l2norm(k) * ksc
            q, k = rotary_xpos(q, k)
            o = local_attention(q, k, v)
            o = o.transpose(0, 2, 1, 3).reshape(b, n, INNER)
            x = x + o @ wo
            h = shift_token(x)
            mu = h.mean(-1, keepdims=True)
            var = h.var(-1, keepdims=True)
            h = (h - mu) / jnp.sqrt(var + 1e-05) * lg + lb
            h = h @ w1 + b1
            a, g = jnp.split(h, 2, axis=-1)
            h = a * jax.nn.gelu(g, approximate=False)
            x = x + h @ w2 + b2
            return x
        for l in range(DEPTH):
            x = _layer(x, wqkv[l], q_scale[l], k_scale[l], wo[l], ln_g[l], ln_b[l], w1[l], b1[l], w2[l], b2[l])
        return x
    x = L0_attn_x
    xn = _layernorm(x, axis=-1)
    s = _L0_attn_ref(xn, L0_attn_W_q, L0_attn_W_k, L0_attn_W_v, L0_attn_W_o)
    g = _silu(_L0_ffn_ref(xn, L0_ffn_wqkv, L0_ffn_q_scale, L0_ffn_k_scale, L0_ffn_wo, L0_ffn_ln_g, L0_ffn_ln_b, L0_ffn_w1, L0_ffn_b1, L0_ffn_w2, L0_ffn_b2))
    x = x + s * g
    return x

_drawn_inputs = setup_inputs


def setup_inputs(seed=0):
    import zlib

    import numpy as np

    out = dict(_drawn_inputs(seed))
    spreads = {'L0_ffn_q_scale': (1.0, 0.6),
     'L0_ffn_k_scale': (1.0, 0.6),
     'L0_ffn_ln_g': (1.0, 0.6),
     'L0_ffn_ln_b': (0.0, 0.8),
     'L0_ffn_b1': (0.0, 0.8),
     'L0_ffn_b2': (0.0, 2.0)}
    factors = {'L0_ffn_wqkv': 8.0, 'L0_ffn_wo': 8.0, 'L0_ffn_w1': 8.0, 'L0_ffn_w2': 8.0}
    for name, (base, spread) in spreads.items():
        noise = np.random.default_rng([zlib.crc32(name.encode()), seed]).standard_normal(out[name].shape)
        drawn = base * np.exp(spread * noise) if base else spread * noise
        out[name] = jnp.asarray(drawn.astype(out[name].dtype))
    for name, factor in factors.items():
        out[name] = (out[name] * factor).astype(out[name].dtype)
    return out
```

```python
import numpy as np
import concourse.bass as bass
from concourse import mybir
from contextlib import ExitStack

F32 = mybir.dt.float32
F32R = mybir.dt.float32r
BF16 = mybir.dt.bfloat16
ALU = mybir.AluOpType
ACT = mybir.ActivationFunctionType
AX = mybir.AxisListType

P = 128
D = 256
KD = D // P
BATCH, SEQ = 4, 1024
TOK = BATCH * SEQ
TILES = TOK // P
TPB = SEQ // P
SUP = 4
SUPERS = TILES // SUP
ST_ROWS = BATCH * (SEQ + 1)
CH, CD = 16, 16
GH = 4
CG = CH // GH
CS = CD ** -0.5
VW = 32
PAIRS = [(0, 0), (0, 1), (0, 2), (1, 0), (1, 1), (2, 0)]
SHIFT_ROW = len(PAIRS) * CD
SROWS = SHIFT_ROW + 2
LAYERS = 2
LH, LD = 8, 64
INNER = LH * LD
KI = INNER // P
HID = 682
HC = 6
QK_SCALE = 8.0
NEG = -1e30
ONE = 1
BIG = 3e38


def stage_row(stage, tile):
    if isinstance(tile, tuple):
        reg, j = tile
        t = reg * 4 + j
    else:
        t = tile
    return stage * ST_ROWS + t * P + t // TPB + 1


def phase_project(nc, K, x, X, QKP, VA, wqk, wv):
    with ExitStack() as c:
        sb = lambda n, s, d: c.enter_context(nc.sbuf_tensor(n, s, d))
        ps = lambda n, s, d: c.enter_context(nc.psum_tensor(n, s, d))
        mine = []

        def sem(name):
            mine.append(c.enter_context(nc.semaphore(name)))
            return mine[-1]

        wst = sb("p1_wst", [P, KD, 768], F32)
        whi = sb("p1_whi", [P, KD, 768], F32R)
        wlo = sb("p1_wlo", [P, KD, 768], F32R)
        xin = sb("p1_xin", [P, 2, SUP, D], F32)
        stt = sb("p1_stt", [P, 2, SUP, 6], F32)
        mv = sb("p1_mv", [P, 2, SUP, 2], F32)
        ve = sb("p1_ve", [P, 2, SUP], F32)
        rstd = sb("p1_rstd", [P, 2, SUP], F32)
        xn = sb("p1_xn", [P, 2, SUP, D], F32)
        thi = sb("p1_thi", [P, 2, KD, SUP * P], F32R)
        tlo = sb("p1_tlo", [P, 2, KD, SUP * P], F32R)
        parts = sb("p1_parts", [P, CG, 3, SUP * P], BF16)
        rest = sb("p1_rest", [P, CG, SUP * P], F32)
        vaug = sb("p1_vaug", [P, 2, SUP, CH, VW], F32)
        pT = ps("p1_pT", [P, KD, 512], F32)
        pQ = ps("p1_pQ", [P, 4, 512], F32)
        pV = ps("p1_pV", [P, 2, 2, D], F32)

        w_loaded, w_hi, w_split = sem("p1_w_loaded"), sem("p1_w_hi"), sem("p1_w_split")
        x_loaded = [sem(f"p1_x_loaded{i}") for i in range(2)]
        stats = sem("p1_stats")
        mv_ready, ve_ready, rstd_ready = sem("p1_mv_ready"), sem("p1_ve_ready"), sem("p1_rstd_ready")
        xn_ready = sem("p1_xn_ready")
        xn_stored = [sem(f"p1_xn_stored{i}") for i in range(2)]
        t_ready, t_hi, t_lo = sem("p1_t_ready"), sem("p1_t_hi"), sem("p1_t_lo")
        q_ready, part0, rest_ready, part1, part2 = (
            sem("p1_q_ready"), sem("p1_part0"), sem("p1_rest_ready"), sem("p1_part1"), sem("p1_part2"))
        part_stored = [sem(f"p1_part_stored{i}") for i in range(CG)]
        v_ready, v_copied, v_preset = sem("p1_v_ready"), sem("p1_v_copied"), sem("p1_v_preset")
        v_stored = [sem(f"p1_v_stored{i}") for i in range(2)]

        x_t = x.rearrange("(s n p) d -> s p n d", n=SUP, p=P)
        va_t = VA.rearrange("(s n p) c -> s p n c", n=SUP, p=P)
        block = c.enter_context(nc.Block())

        def steps(e, first, step, last):
            first()
            with e.Fori(0, SUPERS // 2 - 1) as it:
                for j in range(2):
                    step(it * 2 + j, j, it, False)
            step(SUPERS - 2, 0, SUPERS // 2 - 1, False)
            step(SUPERS - 1, 1, SUPERS // 2 - 1, True)

        @block.sync
        def _(sp):
            sp.dma_start(xin[:, 0], x_t[0]).then_inc(x_loaded[0], 16)
            sp.dma_start(wst[:, :, 0:512], wqk.rearrange("(k p) n -> p k n", p=P)).then_inc(w_loaded, 16)
            sp.dma_start(wst[:, :, 512:768], wv.rearrange("(k p) n -> p k n", p=P)).then_inc(w_loaded, 16)
            sp.dma_start(xin[:, 1], x_t[1]).then_inc(x_loaded[1], 16)

            def store_xn(s, j, it):
                sp.wait_ge(xn_ready, ONE + s + 1)
                row = s * SUP * P + it + 1
                sp.dma_start(X[bass.ds(row, SUP * P), :].rearrange("(n p) d -> p n d", p=P),
                             xn[:, j]).then_inc(xn_stored[j], 16)

            def rest_of(s, j, it):
                for g in range(CG):
                    sp.wait_ge(part2, ONE + CG + s * CG + g + 1)
                    sp.dma_start(QKP[it * CG + g, :, :, j * 512:(j + 1) * 512],
                                 parts[:, g]).then_inc(part_stored[g], 16)
                sp.wait_ge(v_copied, ONE + 2 + s * 2 + 2)
                sp.dma_start(va_t[s], vaug[:, j].rearrange("p n h w -> p n (h w)")).then_inc(v_stored[j], 16)

            def step(s, j, it, final):
                store_xn(s, j, it)
                if not final and not (isinstance(s, int) and s >= SUPERS - 2):
                    sp.dma_start(xin[:, j], x_t[s + 2]).then_inc(x_loaded[j], 16)
                rest_of(s, j, it)

            steps(sp, lambda: None, step, None)
            for j in range(2):
                sp.wait_ge(xn_stored[j], ONE + 16 * SUPERS // 2)
                sp.wait_ge(v_stored[j], ONE + 16 * SUPERS // 2)
            for g in range(CG):
                sp.wait_ge(part_stored[g], ONE + 16 * SUPERS)

        @block.gpsimd
        def _(pool):
            pool.memset(vaug[:, :, :, :, CD + 1:VW], 0.0).then_inc(v_preset, 1)
            pool.memset(vaug[:, :, :, :, CD:CD + 1], 1.0).then_inc(v_preset, 1)

            pool.sem_inc(part2, CG)

            def rstd_of(s, j):
                pool.wait_ge(mv_ready, ONE + (s + 1) * SUP)
                pool.sem_inc(K.passed, 1)
                pool.tensor_scalar(ve[:, j], mv[:, j, :, 1], 1e-5, None, ALU.add).then_inc(ve_ready, 1)
                pool.wait_ge(ve_ready, ONE + s + 1)
                pool.tensor_tensor(rstd[:, j], ve[:, j], K.mhalf[:, 0:SUP], ALU.pow).then_inc(rstd_ready, 1)

            def step(s, j, it, final):
                if not final:
                    rstd_of(s + 1, 1 - j)
                for g in range(CG):
                    pool.wait_ge(part1, ONE + s * CG + g + 1)
                    pool.tensor_tensor(parts[:, g, 2], rest[:, g], parts[:, g, 1],
                                       ALU.subtract).then_inc(part2, 1)

            steps(pool, lambda: rstd_of(0, 0), step, None)

        @block.scalar
        def _(act):
            act.wait_ge(w_loaded, ONE + 32)
            act.activation(whi[:, :, :], wst[:, :, :], ACT.Copy).then_inc(w_hi, 1)

            def hi_of(s, j):
                act.wait_ge(t_ready, ONE + s + 1)
                act.activation(thi[:, j], pT[:, :, :], ACT.Copy).then_inc(t_hi, 1)

            def step(s, j, it, final):
                for g in range(CG):
                    u = s * CG + g
                    act.wait_ge(q_ready, ONE + u + 1)
                    act.wait_ge(part_stored[g], ONE + s * 16)
                    act.activation(parts[:, g, 0], pQ[:, g], ACT.Copy).then_inc(part0, 1)
                    act.wait_ge(rest_ready, ONE + CG + u + 1)
                    act.activation(parts[:, g, 1], rest[:, g], ACT.Copy).then_inc(part1, 1)
                if not final:
                    hi_of(s + 1, 1 - j)

            steps(act, lambda: hi_of(0, 0), step, None)

        @block.vector
        def _(dve):
            start_at_one(dve, mine)
            dve.wait_ge(w_hi, ONE + 1)
            dve.tensor_tensor(wlo[:, :, :], wst[:, :, :], whi[:, :, :].bitcast(F32), ALU.subtract).then_inc(w_split, 1)
            dve.wait_ge(v_preset, ONE + 2)
            dve.sem_inc(rest_ready, CG)
            dve.sem_inc(v_copied, 2)

            def moments(s, j, it):
                dve.wait_ge(x_loaded[j], ONE + (it + 1) * 16)
                for n in range(SUP):
                    dve.bn_stats(stt[:, j, n], xin[:, j, n]).then_inc(stats, 1)
                dve.wait_ge(stats, ONE + s * SUP + SUP)
                dve.sem_inc(K.passed, 1)
                for n in range(SUP):
                    dve.bn_aggr(mv[:, j, n], stt[:, j, n]).then_inc(mv_ready, 1)

            def normalise(s, j, it):
                dve.wait_ge(xn_stored[j], ONE + it * 16)
                dve.wait_ge(rstd_ready, ONE + s + 1)
                for n in range(SUP):
                    ins = dve.tensor_scalar(xn[:, j, n], xin[:, j, n], mv[:, j, n, 0:1], rstd[:, j, n:n + 1],
                                            ALU.subtract, ALU.mult)
                ins.then_inc(xn_ready, 1)

            def lo_of(s, j):
                dve.wait_ge(t_hi, ONE + s + 1)
                dve.tensor_tensor(tlo[:, j], pT[:, :, :], thi[:, j].bitcast(F32), ALU.subtract).then_inc(t_lo, 1)

            def first():
                moments(0, 0, 0)
                normalise(0, 0, 0)
                lo_of(0, 0)

            def step(s, j, it, final):
                if not final:
                    moments(s + 1, 1 - j, it + j)
                for g in range(CG):
                    if g == 2 and not final:
                        normalise(s + 1, 1 - j, it + j)
                    u = s * CG + g
                    dve.wait_ge(part0, ONE + u + 1)
                    dve.wait_ge(part2, ONE + u + 1)
                    dve.tensor_tensor(rest[:, g], pQ[:, g], parts[:, g, 0], ALU.subtract).then_inc(rest_ready, 1)
                if not final:
                    lo_of(s + 1, 1 - j)
                for v in range(2):
                    dve.wait_ge(v_ready, ONE + s * 2 + v + 1)
                    if v == 0:
                        dve.wait_ge(v_stored[j], ONE + it * 16)
                    dve.tensor_copy(vaug[:, j, 2 * v:2 * v + 2, :, 0:CD],
                                    pV[:, v].rearrange("p n (h w) -> p n h w", w=CD)).then_inc(v_copied, 1)

            steps(dve, first, step, None)

        @block.tensor
        def _(pe):
            def transposes(s, j):
                pe.wait_ge(xn_ready, ONE + s + 1)
                pe.wait_ge(t_lo, ONE + s)
                for k in range(KD):
                    for n in range(SUP):
                        ins = pe.transpose(pT[:, k, n * P:(n + 1) * P], xn[:, j, n, k * P:(k + 1) * P], K.ident[:, :])
                ins.then_inc(t_ready, 1)

            def first():
                transposes(0, 0)
                pe.wait_ge(w_split, ONE + 1)

            def step(s, j, it, final):
                pe.wait_ge(t_lo, ONE + s + 1)
                for g in range(CG):
                    pe.wait_ge(rest_ready, ONE + s * CG + g + 1)
                    ws = slice(g * P, (g + 1) * P)
                    terms = [(w, t, k) for k in range(KD) for w, t in ((whi, thi), (whi, tlo), (wlo, thi))]
                    for i, (w, t, k) in enumerate(terms):
                        ins = pe.matmul(pQ[:, g], w[:, k, ws], t[:, j, k], start=i == 0, stop=i == len(terms) - 1)
                    ins.then_inc(q_ready, 1)
                if not final:
                    transposes(s + 1, 1 - j)
                for n in range(SUP):
                    v, o = n // 2, n % 2
                    if o == 0:
                        pe.wait_ge(v_copied, ONE + s * 2 + v + 1)
                    ts = slice(n * P, (n + 1) * P)
                    terms = [(t, w, k) for k in range(KD) for t, w in ((thi, whi), (thi, wlo), (tlo, whi))]
                    for i, (t, w, k) in enumerate(terms):
                        ins = pe.matmul(pV[:, v, o], t[:, j, k, ts], w[:, k, 512:768], start=i == 0, stop=i == len(terms) - 1)
                    if o == 1:
                        ins.then_inc(v_ready, 1)

            steps(pe, first, step, None)


def phase_causal(nc, K, QKP, VA, AO):
    ITERS = BATCH * CG
    RING = 3
    MAXJOBS = [(h, i, ch) for i in range(TPB) for h in range(GH) for ch in range(1 + i // 4)]
    NJ = len(MAXJOBS)
    FIRST = 3
    PER = [2, 4, 5, 5, 5, 6, 6, 6, 6, 0, 0, 0]
    STEPS = [(0, j) for j in range(TPB // 2)] + [(1, j) for j in range(TPB)]
    NSTEP = len(STEPS)
    SHIFT_STEP = 9
    LATE_STEP = 1
    OUT_STEP = 5
    RJ = NJ + 3
    HALF = SEQ // 2
    SLOTS = 3
    LOOPS = (ITERS - 2) // SLOTS

    def plan(started, more):
        at, chunk, index = {}, 0, NJ if started else NJ + 1
        for k in range(-1, NSTEP):
            todo = []
            if more:
                for _ in range(FIRST if k < 0 else PER[k]):
                    todo.append(("max", chunk))
                    chunk += 1
                if k == SHIFT_STEP:
                    todo.append(("shift", 0))
            if k == LATE_STEP and started:
                todo.append(("out", 1))
            if k == OUT_STEP:
                todo.append(("out", 0))
            at[k] = [(index + i, *t) for i, t in enumerate(todo)]
            index += len(todo)
        return at, index

    def span(k):
        half, j = STEPS[k]
        q0 = max(half * HALF, j * P)
        return q0, (half + 1) * HALF - q0

    with ExitStack() as c:
        sb = lambda n, s, d: c.enter_context(nc.sbuf_tensor(n, s, d))
        ps = lambda n, s, d: c.enter_context(nc.psum_tensor(n, s, d))
        mine = []

        def sem(name):
            mine.append(c.enter_context(nc.semaphore(name)))
            return mine[-1]

        qs = sb("ca_qs", [SROWS, SLOTS, GH, SEQ], BF16)
        ks = sb("ca_ks", [SROWS, SLOTS, GH, SEQ], BF16)
        va = sb("ca_va", [P, SLOTS, TPB, GH * VW], F32)
        mask_q = sb("ca_mask_q", [P, P], BF16)
        mask_k = sb("ca_mask_k", [P, P], BF16)
        mx = sb("ca_mx", [P, TPB, GH, 2], F32)
        nm = sb("ca_nm", [P, TPB, GH], F32)
        nms = sb("ca_nms", [P, TPB, 2, GH], BF16)
        shift = sb("ca_shift", [2 * GH, SEQ], BF16)
        pr = sb("ca_pr", [P, 2, 2, 2, 512], F32)
        ot = sb("ca_ot", [P, 2, 512], F32)
        rec = sb("ca_rec", [P, 2, SUP, GH], F32)
        att = sb("ca_att", [P, 2, SUP, GH, CD], F32)
        pS = ps("ca_pS", [P, 2, 2, 512], F32)
        pR = [ps(f"ca_pR{i}", [P, 512], F32) for i in range(RING)]
        pO = ps("ca_pO", [P, 512], F32)

        made, ones = sem("ca_made"), sem("ca_ones")
        loaded = [sem(f"ca_loaded{i}") for i in range(SLOTS)]
        shifted = [sem(f"ca_shifted{i}") for i in range(SLOTS)]
        ring_full, ring_free = sem("ca_ring_full"), sem("ca_ring_free")
        min_done, hi_done, split_done = sem("ca_min_done"), sem("ca_hi_done"), sem("ca_split_done")
        s_ready, p_ready, pv_done = sem("ca_s_ready"), sem("ca_p_ready"), sem("ca_pv_done")
        ot_copied, rec_done = sem("ca_ot_copied"), sem("ca_rec_done")
        att_stored = [sem(f"ca_att_stored{i}") for i in range(2)]

        va_t = VA.rearrange("(b t p) (g c) -> b g p t c", b=BATCH, p=P, g=CG)
        ao_t = AO.rearrange("(b f t p) (g c) -> b f g p t c", b=BATCH, f=2, p=P, g=CG)
        LOADS = 2 * len(PAIRS) + 1
        block = c.enter_context(nc.Block())

        def run(e, first, step):
            first()
            step(0, 0, 0, False, True)
            with e.Fori(0, LOOPS) as it:
                for u in range(1, SLOTS + 1):
                    step(it * SLOTS + u, u % SLOTS, it + u // SLOTS, True, True)
            for n in range(LOOPS * SLOTS + 1, ITERS):
                step(n, n % SLOTS, n // SLOTS, True, n < ITERS - 1)

        @block.gpsimd
        def _(pool):
            pool.memset(mask_q[:, :], 0.0).then_inc(made, 1)
            pool.memset(mask_k[:, :], 0.0).then_inc(made, 1)
            pool.memset(mx[:, :, :, :], BIG).then_inc(made, 1)
            pool.wait_ge(made, ONE + 3)
            pool.affine_select(out=mask_q[:, :], in_=mask_q[:, :], compare_op=ALU.is_ge, fill=NEG,
                               base=0, pattern=[[-1, P]], channel_multiplier=1).then_inc(made, 1)
            pool.affine_select(out=mask_k[:, :], in_=mask_k[:, :], compare_op=ALU.is_ge, fill=NEG,
                               base=0, pattern=[[1, P]], channel_multiplier=-1).then_inc(made, 1)
            pool.wait_ge(made, ONE + 5)
            for u in range(SLOTS):
                pool.memset(ks[SHIFT_ROW:SROWS, u, :, :], 1.0).then_inc(ones, 1)
                pool.wait_ge(ones, ONE + u + 1)

        @block.sync
        def _(sp):
            def load(n, u):
                b, g = n // CG, n % CG
                for r, (a, k) in enumerate(PAIRS):
                    rows = slice(r * CD, (r + 1) * CD)
                    src = QKP[n].rearrange("(z h d) c s -> z c d h s", z=2, h=GH)
                    sp.dma_start(qs[rows, u], src[0, a]).then_inc(loaded[u], 16)
                    sp.dma_start(ks[rows, u], src[1, k]).then_inc(loaded[u], 16)
                sp.dma_start(va[:, u], va_t[b, g]).then_inc(loaded[u], 16)

            def place_shift(u, jobs):
                sp.wait_ge(ring_free, ONE + RING + jobs)
                for part in range(2):
                    sp.dma_start(qs[SHIFT_ROW + part:SHIFT_ROW + part + 1, u, :, :],
                                 shift[part * GH:(part + 1) * GH, :]).then_inc(shifted[u], 16)

            def store(n, half, jobs):
                sp.wait_ge(ring_free, ONE + RING + jobs)
                sp.dma_start(ao_t[n // CG, half, n % CG], att[:, half].rearrange("p t h d -> p t (h d)"))\
                  .then_inc(att_stored[half], 16)

            def first():
                for n in range(SLOTS):
                    load(n, n)
                place_shift(0, NJ + 1)

            def step(n, u, it, started, more):
                at, _ = plan(started, more)
                for job, kind, half in sum(at.values(), []):
                    if kind == "out":
                        store(n - half, half, n * RJ + job + 1)
                    elif kind == "shift":
                        place_shift((u + 1) % SLOTS, n * RJ + job + 1)
                    if kind == "out" and half == 1 and not (isinstance(n, int) and n - 1 + SLOTS >= ITERS):
                        load(n - 1 + SLOTS, (u - 1) % SLOTS)

            run(sp, first, step)
            store(ITERS - 1, 1, (ITERS - 1) * RJ + NJ + 3)
            for half in range(2):
                sp.wait_ge(att_stored[half], ONE + ITERS * 16)

        @block.tensor
        def _(pe):
            def ring(job, n):
                pe.wait_ge(ring_free, ONE + n * RJ + job + 1)
                return pR[job % RING]

            def maxima(idx, n, u, job):
                h, i, ch = MAXJOBS[idx]
                k0 = ch * 512
                w = min((i + 1) * P - k0, 512)
                bank = ring(*job)
                diag = k0 + w == (i + 1) * P
                ins = pe.matmul(bank[:, 0:w], qs[0:SHIFT_ROW, u, h, i * P:(i + 1) * P],
                                ks[0:SHIFT_ROW, u, h, k0:k0 + w], start=True, stop=not diag)
                if diag:
                    ins = pe.matmul(bank[:, w - P:w], K.identb[:, :], mask_q[:, :], start=False, stop=True)
                ins.then_inc(ring_full, 1)

            def turn_shift(n, job):
                pe.wait_ge(split_done, ONE + n + 1)
                view = ring(*job)[0:2 * GH, :].bitcast(BF16)
                for i in range(TPB):
                    ins = pe.transpose(view[:, i * P:(i + 1) * P], nms[:, i].rearrange("p a h -> p (a h)"),
                                       K.identb[:, :])
                ins.then_inc(ring_full, 1)

            def scores(n, u, k, pairs=range(2)):
                half, j = STEPS[k]
                q0, w = span(k)
                for pair in pairs:
                    pe.wait_ge(p_ready, ONE + n * 2 * NSTEP + 2 * k + pair + 1)
                    for hh in range(2):
                        h = pair * 2 + hh
                        diag = j * P >= half * HALF
                        ins = pe.matmul(pS[:, pair, hh, 0:w], ks[:, u, h, j * P:(j + 1) * P],
                                        qs[:, u, h, q0:q0 + w], start=True, stop=not diag)
                        if diag:
                            ins = pe.matmul(pS[:, pair, hh, 0:P], K.identb[:, :], mask_k[:, :], start=False, stop=True)
                    ins.then_inc(s_ready, 1)

            def weighted(n, u, k):
                half, j = STEPS[k]
                q0, w = span(k)
                o = q0 - half * HALF
                pe.wait_ge(p_ready, ONE + 2 + n * 2 * NSTEP + 2 * k + 2)
                if j == 0:
                    pe.wait_ge(ot_copied, ONE + n * 2 + half)
                last = j == (half + 1) * (TPB // 2) - 1
                for h in range(GH):
                    ins = pe.matmul(pO[h * VW:(h + 1) * VW, o:o + w], va[:, u, j, h * VW:(h + 1) * VW],
                                    pr[:, k % 2, h // 2, h % 2, 0:w], start=j == 0, stop=last)
                ins.then_inc(pv_done, 1)

            def turn_out(n, half, job):
                pe.wait_ge(ot_copied, ONE + n * 2 + half + 1)
                bank = ring(*job)
                for t in range(SUP):
                    ins = pe.transpose(bank[:, t * P:(t + 1) * P], ot[:, half, t * P:(t + 1) * P], K.ident[:, :])
                ins.then_inc(ring_full, 1)

            def first():
                pe.wait_ge(loaded[0], ONE + LOADS * 16)
                for idx in range(NJ):
                    maxima(idx, 0, 0, (idx, 0))
                turn_shift(0, (NJ, 0))

            def step(n, u, it, started, more):
                at, _ = plan(started, more)

                def do(jobs):
                    for job, kind, which in jobs:
                        if kind == "max":
                            maxima(which, n + 1, (u + 1) % SLOTS, (job, n))
                        elif kind == "shift":
                            turn_shift(n + 1, (job, n))
                        else:
                            turn_out(n - which, which, (job, n))

                if more:
                    pe.wait_ge(loaded[(u + 1) % SLOTS], ONE + (it + 1 + (u + 1) // SLOTS) * LOADS * 16)
                do(at[-1])
                if not started:
                    pe.wait_ge(ones, ONE + SLOTS)
                pe.wait_ge(shifted[u], ONE + (it + 1) * 2 * 16)
                for k in range(NSTEP):
                    scores(n, u, k, [0])
                    do(at[k][:2])
                    scores(n, u, k, [1])
                    do(at[k][2:4])
                    if k:
                        weighted(n, u, k - 1)
                    elif started:
                        weighted(n - 1, (u - 1) % SLOTS, NSTEP - 1)
                    do(at[k][4:])

            pe.wait_ge(made, ONE + 5)
            run(pe, first, step)
            weighted(ITERS - 1, (ITERS - 1) % SLOTS, NSTEP - 1)
            turn_out(ITERS - 1, 1, (NJ + 2, ITERS - 1))

        @block.scalar
        def _(act):
            def step(n, u, it, started, more):
                for k in range(NSTEP):
                    q0, w = span(k)
                    for pair in range(2):
                        act.wait_ge(s_ready, ONE + n * 2 * NSTEP + 2 * k + pair + 1)
                        act.wait_ge(pv_done, ONE + n * NSTEP + max(k - 1, 0))
                        act.activation(pr[:, k % 2, pair, :, 0:w], pS[:, pair, :, 0:w], ACT.Exp,
                                       scale=CS).then_inc(p_ready, 1)
                    if k == 0 and started:
                        copy_out(n - 1, 1)
                    if k == TPB // 2:
                        copy_out(n, 0)

            def copy_out(n, half):
                act.wait_ge(pv_done, ONE + n * NSTEP + (TPB // 2, NSTEP)[half])
                act.activation(ot[:, half], pO[:, :], ACT.Copy).then_inc(ot_copied, 1)

            act.sem_inc(p_ready, 2)
            run(act, lambda: None, step)
            copy_out(ITERS - 1, 1)

        @block.vector
        def _(dve):
            start_at_one(dve, mine)
            def take_max(idx, job):
                h, i, ch = MAXJOBS[idx]
                w = min((i + 1) * P - ch * 512, 512)
                jb, n = job
                dve.wait_ge(ring_full, ONE + n * RJ + jb + 1)
                dve.tensor_reduce(mx[:, i, h, ch:ch + 1], pR[jb % RING][:, 0:w], AX.X, ALU.max,
                                  negate=True).then_inc(ring_free, 1)

            def split(n, jobs_before):
                dve.wait_ge(ring_free, ONE + RING + jobs_before)
                dve.tensor_tensor(nm[:, :, :], mx[:, :, :, 0], mx[:, :, :, 1], ALU.min).then_inc(min_done, 1)
                dve.wait_ge(min_done, ONE + n + 1)
                dve.tensor_copy(nms[:, :, 0], nm[:, :, :]).then_inc(hi_done, 1)
                dve.wait_ge(hi_done, ONE + n + 1)
                dve.tensor_tensor(nms[:, :, 1], nm[:, :, :], nms[:, :, 0], ALU.subtract).then_inc(split_done, 1)

            def take_shift(job):
                jb, m = job
                dve.wait_ge(ring_full, ONE + m * RJ + jb + 1)
                dve.tensor_copy(shift[:, :], pR[jb % RING][0:2 * GH, :].bitcast(BF16)).then_inc(ring_free, 1)

            def take_out(n, half, job):
                jb, m = job
                dve.wait_ge(ring_full, ONE + m * RJ + jb + 1)
                v = pR[jb % RING][:, :].rearrange("p (t h c) -> p t h c", t=SUP, h=GH)
                dve.reciprocal(rec[:, half], v[:, :, :, CD]).then_inc(rec_done, 1)
                dve.wait_ge(rec_done, ONE + n * 2 + half + 1)
                dve.wait_ge(att_stored[half], ONE + n * 16)
                dve.tensor_tensor(att[:, half], v[:, :, :, 0:CD],
                                  rec[:, half, :, :, None].broadcast_to([P, SUP, GH, CD]),
                                  ALU.mult).then_inc(ring_free, 1)

            def first():
                for idx in range(NJ):
                    take_max(idx, (idx, 0))
                split(0, NJ)
                take_shift((NJ, 0))

            def step(n, u, it, started, more):
                at, _ = plan(started, more)
                for job, kind, which in sum(at.values(), []):
                    if kind == "max":
                        take_max(which, (job, n))
                        if which == NJ - 1:
                            split(n + 1, n * RJ + job + 1)
                    elif kind == "shift":
                        dve.wait_ge(shifted[u], ONE + (it + 1) * 2 * 16)
                        take_shift((job, n))
                    else:
                        take_out(n - which, which, (job, n))

            dve.wait_ge(made, ONE + 5)
            dve.sem_inc(ring_free, RING)
            run(dve, first, step)
            take_out(ITERS - 1, 1, (NJ + 2, ITERS - 1))


def phase_window(nc, K, W, layer, X, wqkv, wo, q_scale, k_scale):
    NW = TILES
    (wo_st, wo_hi, wo_lo, scales, tab, xt, hs, thi, tlo, qk, sq, ss, ssc, rs,
     tc, tsn, rr, qkn, v, kt, qz, nmax, sums, rsum, pe_, pn, pt, oth, otl, x1, pX, pS) = W.tensors
    qkv_st, qkv_hi, qkv_lo = W.weights
    base, masks = K.base, K.masks
    S = W.sems
    g0 = layer * NW

    def steps(e, step):
        with e.Fori(0, NW // 4 - 1) as it:
            for j in range(4):
                step(it * 4 + j, j, it)
        for j in range(4):
            step(NW - 4 + j, j, NW // 4 - 1)

    def ahead(w, j, it, n):
        if isinstance(w, int) and w + n >= NW:
            return None
        return w + n, (j + n) % 4, it + (j + n) // 4

    with nc.Block() as block:
        @block.sync
        def _(sp):
            sp.dma_start(qkv_st[:, :, :], wqkv[layer].rearrange("(k p) n -> p k n", p=P)).then_inc(S["w_loaded"], 16)
            sp.dma_start(wo_st[:, :, :], wo[layer].rearrange("(k p) n -> p k n", p=P)).then_inc(S["w_loaded"], 16)
            for i, src in enumerate((q_scale, k_scale)):
                for r in range(2):
                    row = src[layer]
                    for hf in range(2):
                        o = (hf ^ r) * (LD // 2)
                        sp.dma_start(scales[:, 2 * i + r, hf * (LD // 2):(hf + 1) * (LD // 2)],
                                     row[o:o + LD // 2][None, :].broadcast_to([P, LD // 2])).then_inc(S["w_loaded"], 16)

            def load(w, j, it):
                r0 = stage_row(2 * layer, w)
                sp.dma_start(xt[:, j], X[bass.ds(r0, P), :]).then_inc(S["x_loaded"][j], 16)
                sp.dma_start(hs[:, j], X[bass.ds(r0 - 1, P), P:D]).then_inc(S["x_loaded"][j], 16)

            for w in range(4):
                load(w, w, 0)

            def step(w, j, it):
                sp.wait_ge(S["x1_ready"], ONE + 2 + g0 + w + 1)
                sp.dma_start(X[bass.ds(stage_row(2 * layer + 1, w), P), :], x1[:, j % 2])\
                  .then_inc(S["x1_stored"][j % 2], 16)
                nxt = ahead(w, j, it, 4)
                if nxt:
                    load(*nxt)

            steps(sp, step)
            for i in range(2):
                sp.wait_ge(S["x1_stored"][i], ONE + (layer + 1) * (NW // 2) * 16)
            sp.sem_inc(K.passed, 1)

        @block.gpsimd
        def _(pool):
            def squares(w, j, it):
                pool.wait_ge(S["k_copied"], ONE + g0 + w + 1)
                pool.wait_ge(S["ss_ready"], ONE + g0 + w)
                pool.tensor_tensor(sq[:, :], qk[:, j % 2], qk[:, j % 2], ALU.mult).then_inc(S["sq_ready"], 1)

            def rotated(w, j, it):
                pool.wait_ge(S["added"], ONE + g0 + w)
                t = w % TPB
                for z in range(2):
                    src = qk[:, j % 2, z * INNER:(z + 1) * INNER].rearrange("p (h f d) -> p h f d", f=2, d=LD // 2)
                    dst = tsn[:, z * INNER:(z + 1) * INNER].rearrange("p (h f d) -> p h f d", f=2, d=LD // 2)
                    s = tab[:, t, 2 * z + 1].rearrange("p (f d) -> p f d", f=2)[:, None].broadcast_to([P, LH, 2, LD // 2])
                    pool.tensor_tensor(dst, src[:, :, ::-1, :], s, ALU.mult).then_inc(S["ts_ready"], 1)
                pool.wait_ge(S["ss_ready"], ONE + g0 + w + 1)
                pool.sem_inc(K.passed, 1)
                pool.tensor_scalar(ssc[:, :], ss[:, j % 2], 1e-24, None, ALU.max).then_inc(S["ssc_ready"], 1)
                pool.wait_ge(S["ssc_ready"], ONE + g0 + w + 1)
                pool.tensor_tensor(rs[:, j % 2], ssc[:, :], K.mhalf[:, :], ALU.pow).then_inc(S["rs_ready"], 1)

            def rope(nxt):
                if nxt:
                    squares(*nxt)
                    rotated(*nxt)

            pool.memset(qz[:, :, :], 0.0).then_inc(S["cleared"], 1)
            pool.memset(kt[:, :, 1], 0.0).then_inc(S["cleared"], 1)
            pool.memset(v[:, 3], 0.0).then_inc(S["cleared"], 1)
            pool.wait_ge(S["tab_ready"], ONE + layer + 1)
            rope((0, 0, 0))
            rope((1, 1, 0))

            def step(w, j, it):
                rope(ahead(w, j, it, 2))

            steps(pool, step)

        @block.scalar
        def _(act):
            act.wait_ge(S["w_loaded"], ONE + (layer + 1) * 10 * 16)
            act.activation(qkv_hi[:, :, :], qkv_st[:, :, :], ACT.Copy).then_inc(S["w_hi"], 1)
            act.activation(wo_hi[:, :, :], wo_st[:, :, :], ACT.Copy).then_inc(S["w_hi"], 1)

            def turned(w, j, it):
                act.wait_ge(S["t_ready"], ONE + g0 + w + 1)
                act.activation(thi[:, j % 2], pX[:, 0, 0:D].rearrange("p (k t) -> p k t", k=KD), ACT.Copy)\
                   .then_inc(S["t_hi"], 1)

            def copy_q(w, j, it):
                act.wait_ge(S["q_ready"], ONE + g0 + w + 1)
                act.activation(qk[:, j % 2, 0:INNER], pX[:, 1], ACT.Copy).then_inc(S["q_copied"], 1)

            def copy_k(w, j, it):
                act.wait_ge(S["k_ready"], ONE + g0 + w + 1)
                act.activation(qk[:, j % 2, INNER:2 * INNER], pX[:, 2], ACT.Copy).then_inc(S["k_copied"], 1)

            def exps(w, j, it, hf):
                act.wait_ge(S["max_ready"], ONE + 2 * (g0 + w) + hf + 1)
                for h in range(4 * hf, 4 * hf + 4):
                    ins = act.activation(pe_[:, h], pS[:, h // 2, h % 2], ACT.Exp, bias=nmax[:, h:h + 1],
                                         accum_out=sums[:, h:h + 1])
                ins.then_inc(S["exp_done"], 1)

            def copy_p(w, j, it, ch):
                act.wait_ge(S["pt_ready"], ONE + 4 * (g0 + w) + ch + 1)
                act.activation(pt[:, ch], pX[:, (0, 1, 3, 0)[ch]], ACT.Copy).then_inc(S["pt_even"], 1)

            def copy_kt(w, j, it):
                act.wait_ge(S["kt_ready"], ONE + g0 + w + 1)
                act.activation(kt[:, :, j % 2], pX[:, 1].rearrange("p (c t) -> p c t", c=4), ACT.Copy)\
                   .then_inc(S["kt_copied"], 1)

            def copy_v(w, j, it):
                act.wait_ge(S["v_ready"], ONE + g0 + w + 1)
                act.activation(v[:, j], pX[:, 3], ACT.Copy).then_inc(S["v_copied"], 1)

            def copy_qz(w, j, it):
                act.wait_ge(S["qt_ready"], ONE + g0 + w + 1)
                for r in range(2):
                    rows = slice(r * LD, (r + 1) * LD)
                    ins = act.activation(qz[rows, r:LH:2, :], pX[rows, 3].rearrange("p (c t) -> p c t", c=4), ACT.Copy)
                ins.then_inc(S["qt_copied"], 1)

            act.wait_ge(S["cleared"], ONE + 3 * layer + 3)
            for w in range(2):
                turned(w, w, 0)
                copy_q(w, w, 0)
                copy_k(w, w, 0)
                copy_v(w, w, 0)
            copy_kt(0, 0, 0)
            copy_qz(0, 0, 0)
            turned(2, 2, 0)

            def step(w, j, it):
                a2 = ahead(w, j, it, 2)
                a1 = ahead(w, j, it, 1)
                a3 = ahead(w, j, it, 3)
                exps(w, j, it, 0)
                if a2:
                    copy_q(*a2)
                exps(w, j, it, 1)
                if a2:
                    copy_k(*a2)
                    copy_v(*a2)
                copy_p(w, j, it, 0)
                copy_p(w, j, it, 2)
                act.wait_ge(S["ot_ready"], ONE + g0 + w + 1)
                act.activation(oth[:, :], pX[:, 2], ACT.Copy).then_inc(S["ot_hi"], 1)
                if a1:
                    copy_kt(*a1)
                    copy_qz(*a1)
                if a3:
                    turned(*a3)

            steps(act, step)

        @block.vector
        def _(dve):
            dve.wait_ge(S["w_hi"], ONE + 2 * layer + 2)
            dve.tensor_tensor(qkv_lo[:, :, :], qkv_st[:, :, :], qkv_hi[:, :, :].bitcast(F32), ALU.subtract)\
               .then_inc(S["w_split"], 1)
            dve.tensor_tensor(wo_lo[:, :, :], wo_st[:, :, :], wo_hi[:, :, :].bitcast(F32), ALU.subtract)\
               .then_inc(S["w_split"], 1)
            dve.tensor_tensor(tab[:, :, :, :].rearrange("p t f d -> p t (f d)"),
                              base[:, :, :, :].rearrange("p t f d -> p t (f d)"),
                              scales[:, :, :].rearrange("p f d -> p (f d)")[:, None, :].broadcast_to([P, TPB, 4 * LD]),
                              ALU.mult).then_inc(S["tab_ready"], 1)

            def lo_of(w, j, it):
                dve.wait_ge(S["t_hi"], ONE + g0 + w + 1)
                dve.tensor_tensor(tlo[:, j % 2], pX[:, 0, 0:D].rearrange("p (k t) -> p k t", k=KD),
                                  thi[:, j % 2].bitcast(F32), ALU.subtract).then_inc(S["t_lo"], 1)

            def cosines(w, j, it):
                dve.wait_ge(S["k_copied"], ONE + g0 + w + 1)
                dve.wait_ge(S["added"], ONE + g0 + w)
                t = w % TPB
                c = tab[:, t].rearrange("p (z f) d -> p z f d", z=2)[:, :, 0][:, :, None, :].broadcast_to([P, 2, LH, LD])
                dve.tensor_tensor(tc[:, :].rearrange("p (z h d) -> p z h d", z=2, h=LH),
                                  qk[:, j % 2].rearrange("p (z h d) -> p z h d", z=2, h=LH), c, ALU.mult)\
                   .then_inc(S["tc_ready"], 1)

            def sum_squares(w, j, it):
                dve.wait_ge(S["sq_ready"], ONE + g0 + w + 1)
                dve.wait_ge(S["ssc_ready"], ONE + g0 + w)
                dve.tensor_reduce(ss[:, j % 2], sq[:, :].rearrange("p (h d) -> p h d", d=LD), AX.X, ALU.add)\
                   .then_inc(S["ss_ready"], 1)

            def add(w, j, it):
                dve.wait_ge(S["tc_ready"], ONE + g0 + w + 1)
                dve.wait_ge(S["ts_ready"], ONE + 2 * (g0 + w) + 2)
                dve.wait_ge(S["qkn_ready"], ONE + g0 + w)
                dve.tensor_tensor(rr[:, :], tc[:, :], tsn[:, :], ALU.add).then_inc(S["added"], 1)

            def unit(w, j, it):
                dve.wait_ge(S["added"], ONE + g0 + w + 1)
                dve.wait_ge(S["rs_ready"], ONE + g0 + w + 1)
                dve.tensor_tensor(qkn[:, :].rearrange("p (h d) -> p h d", d=LD),
                                  rr[:, :].rearrange("p (h d) -> p h d", d=LD),
                                  rs[:, j % 2][:, :, None].broadcast_to([P, 2 * LH, LD]), ALU.mult)\
                   .then_inc(S["qkn_ready"], 1)

            def maxima(w, j, it, hf):
                dve.wait_ge(S["s_ready"], ONE + 2 * (g0 + w) + hf + 1)
                dve.tensor_reduce(nmax[:, 4 * hf:4 * hf + 4],
                                  pS[:, 2 * hf:2 * hf + 2].rearrange("p b h k -> p (b h) k"), AX.X, ALU.max,
                                  negate=True).then_inc(S["max_ready"], 1)

            def normalise(w, j, it, hf):
                dve.wait_ge(S["exp_done"], ONE + 2 + 2 * (g0 + w) + hf + 1)
                dve.reciprocal(rsum[:, 4 * hf:4 * hf + 4], sums[:, 4 * hf:4 * hf + 4]).then_inc(S["rsum_ready"], 1)
                dve.wait_ge(S["rsum_ready"], ONE + 2 * (g0 + w) + hf + 1)
                for h in range(4 * hf, 4 * hf + 4):
                    ins = dve.tensor_scalar(pn[:, h], pe_[:, h], rsum[:, h:h + 1], None, ALU.mult)
                ins.then_inc(S["pn_ready"], 1)

            def copy_p(w, j, it, ch):
                dve.wait_ge(S["pt_ready"], ONE + 4 * (g0 + w) + ch + 1)
                dve.tensor_copy(pt[:, ch], pX[:, (0, 1, 3, 0)[ch]]).then_inc(S["pt_odd"], 1)

            def lo_out(w, j, it):
                dve.wait_ge(S["ot_hi"], ONE + g0 + w + 1)
                dve.tensor_tensor(otl[:, :], pX[:, 2], oth[:, :].bitcast(F32), ALU.subtract).then_inc(S["ot_lo"], 1)

            def residual(w, j, it):
                dve.wait_ge(S["wo_ready"], ONE + g0 + w + 1)
                dve.wait_ge(S["x1_stored"][j % 2], ONE + (layer * (NW // 2) + (w // 2)) * 16)
                dve.tensor_tensor(x1[:, j % 2], pX[:, 0, 0:D], xt[:, j], ALU.add).then_inc(S["x1_ready"], 1)

            dve.wait_ge(S["cleared"], ONE + 3 * layer + 3)
            for w in range(2):
                lo_of(w, w, 0)
                cosines(w, w, 0)
                sum_squares(w, w, 0)
                add(w, w, 0)
                if w == 0:
                    unit(0, 0, 0)
            maxima(0, 0, 0, 0)
            lo_of(2, 2, 0)
            maxima(0, 0, 0, 1)

            def step(w, j, it):
                a1, a2, a3 = (ahead(w, j, it, n) for n in (1, 2, 3))
                if a1:
                    unit(*a1)
                normalise(w, j, it, 0)
                normalise(w, j, it, 1)
                copy_p(w, j, it, 1)
                copy_p(w, j, it, 3)
                lo_out(w, j, it)
                if a2:
                    cosines(*a2)
                residual(w, j, it)
                if a2:
                    sum_squares(*a2)
                    add(*a2)
                if a1:
                    maxima(*a1, 0)
                if a3:
                    lo_of(*a3)
                if a1:
                    maxima(*a1, 1)

            steps(dve, step)

        @block.tensor
        def _(pe):
            def turn_h(w, j, it):
                pe.wait_ge(S["x_loaded"][j], ONE + (layer * (NW // 4) + it + 1) * 32)
                pe.wait_ge(S["x1_ready"], ONE + g0 + w)
                pe.wait_ge(S["t_lo"], ONE + g0 + w)
                pe.transpose(pX[:, 0, 0:P], xt[:, j, 0:P], K.ident[:, :])
                pe.transpose(pX[:, 0, P:D], hs[:, j], K.ident[:, :]).then_inc(S["t_ready"], 1)

            def project(w, j, it):
                pe.wait_ge(S["t_lo"], ONE + g0 + w + 1)
                for z in range(3):
                    if z == 0:
                        pe.wait_ge(S["kt_copied"], ONE + g0 + w)
                        pe.wait_ge(S["q_copied"], ONE + g0 + w)
                    elif z == 1:
                        pe.wait_ge(S["ot_lo"], ONE + g0 + w)
                        pe.wait_ge(S["k_copied"], ONE + g0 + w)
                    else:
                        pe.wait_ge(S["qt_copied"], ONE + g0 + w)
                        pe.wait_ge(S["v_copied"], ONE + g0 + w)
                    cols = slice(z * INNER, (z + 1) * INNER)
                    terms = [(t, m, k) for k in range(KD) for t, m in ((thi, qkv_hi), (thi, qkv_lo), (tlo, qkv_hi))]
                    for i, (t, m, k) in enumerate(terms):
                        ins = pe.matmul(pX[:, 1 + z], t[:, j % 2, k], m[:, k, cols], start=i == 0,
                                        stop=i == len(terms) - 1)
                    ins.then_inc((S["q_ready"], S["k_ready"], S["v_ready"])[z], 1)

            def turn_p(w, j, it, ch, bank):
                pe.wait_ge(S["pn_ready"], ONE + 2 * (g0 + w) + ch // 2 + 1)
                for hh in range(2):
                    for s in range(2):
                        o = (2 * hh + s) * P
                        ins = pe.transpose(pX[:, bank, o:o + P], pn[:, 2 * ch + hh, s * P:(s + 1) * P], K.ident[:, :])
                ins.then_inc(S["pt_ready"], 1)

            def values(w, j, it, ch):
                if ch % 2 == 0:
                    pe.wait_ge(S["pt_even"], ONE + 2 * (g0 + w) + ch // 2 + 1)
                else:
                    pe.wait_ge(S["pt_odd"], ONE + 2 * (g0 + w) + ch // 2 + 1)
                for s in range(2):
                    vj = j if s == j % 2 else (j - 1) % 4
                    for hh in range(2):
                        h, o = 2 * ch + hh, (2 * hh + s) * P
                        ins = pe.matmul(pX[hh * LD:(hh + 1) * LD, 2, ch * P:(ch + 1) * P], v[:, vj, h * LD:(h + 1) * LD],
                                        pt[:, ch, o:o + P], start=s == 0, stop=s == 1)
                if ch == 3:
                    ins.then_inc(S["ot_ready"], 1)

            def attend(w, j, it):
                last = min(w + 3, NW) if isinstance(w, int) else w + 3
                pe.wait_ge(S["x1_ready"], ONE + 2 + g0 + w)
                turn_p(w, j, it, 0, 0)
                pe.wait_ge(S["q_copied"], ONE + g0 + last)
                pe.wait_ge(S["kt_copied"], ONE + 1 + g0 + w + 1)
                turn_p(w, j, it, 1, 1)
                pe.wait_ge(S["k_copied"], ONE + g0 + last)
                pe.wait_ge(S["ot_lo"], ONE + 2 + g0 + w)
                values(w, j, it, 0)
                pe.wait_ge(S["v_copied"], ONE + g0 + last)
                pe.wait_ge(S["qt_copied"], ONE + 1 + g0 + w + 1)
                turn_p(w, j, it, 2, 3)
                values(w, j, it, 1)
                turn_p(w, j, it, 3, 0)
                values(w, j, it, 2)
                values(w, j, it, 3)

            def turn_qk(w, j, it):
                last = min(w + 2, NW) if isinstance(w, int) else w + 2
                pe.wait_ge(S["qkn_ready"], ONE + g0 + w + 1)
                pe.wait_ge(S["q_copied"], ONE + g0 + last)
                for ch in range(4):
                    ins = pe.transpose(pX[:, 1, ch * P:(ch + 1) * P], qkn[:, INNER + ch * P:INNER + (ch + 1) * P],
                                       K.ident[:, :])
                ins.then_inc(S["kt_ready"], 1)
                pe.wait_ge(S["v_copied"], ONE + g0 + last)
                for ch in range(4):
                    ins = pe.transpose(pX[:, 3, ch * P:(ch + 1) * P], qkn[:, ch * P:(ch + 1) * P], K.ident[:, :])
                ins.then_inc(S["qt_ready"], 1)

            def output(w, j, it):
                pe.wait_ge(S["ot_lo"], ONE + 2 + g0 + w + 1)
                terms = [(t, m, k) for k in range(KI) for t, m in ((oth, wo_hi), (oth, wo_lo), (otl, wo_hi))]
                for i, (t, m, k) in enumerate(terms):
                    ins = pe.matmul(pX[:, 0, 0:D], t[:, k * P:(k + 1) * P], m[:, k], start=i == 0,
                                    stop=i == len(terms) - 1)
                ins.then_inc(S["wo_ready"], 1)

            def score(w, j, it, hf):
                if hf == 0:
                    pe.wait_ge(S["kt_copied"], ONE + 1 + g0 + w + 1)
                    pe.wait_ge(S["qt_copied"], ONE + 1 + g0 + w + 1)
                pe.wait_ge(S["exp_done"], ONE + 2 * (g0 + w) + hf + 1)
                kind = it % 2 if j == 0 else (2 if j % 2 else 1)
                for b in (2 * hf, 2 * hf + 1):
                    pe.matmul(pS[:, b].rearrange("p h k -> p (h k)"), K.identb[:, :], masks[:, kind], start=True,
                              stop=False)
                    for hh in range(2):
                        ins = pe.matmul(pS[:, b, hh], qz[:, 2 * b + hh, :], kt[:, b].rearrange("p s t -> p (s t)"),
                                        start=False, stop=hh == 1)
                ins.then_inc(S["s_ready"], 1)

            pe.wait_ge(S["w_split"], ONE + 2 * layer + 2)
            pe.wait_ge(S["cleared"], ONE + 3 * layer + 3)
            for w in range(2):
                turn_h(w, w, 0)
                project(w, w, 0)
            turn_qk(0, 0, 0)
            score(0, 0, 0, 0)
            turn_h(2, 2, 0)
            score(0, 0, 0, 1)

            def step(w, j, it):
                a1, a2, a3 = (ahead(w, j, it, n) for n in (1, 2, 3))
                if a2:
                    project(*a2)
                attend(w, j, it)
                if a1:
                    turn_qk(*a1)
                output(w, j, it)
                if a1:
                    score(*a1, 0)
                if a3:
                    turn_h(*a3)
                if a1:
                    score(*a1, 1)

            steps(pe, step)


def phase_feed(nc, K, W, F, layer, X, ln_g, ln_b, w1, b1, w2, b2):
    NS = SUPERS
    N = SUP * P
    HA = HC * P
    TAIL = HID - (HC - 1) * P
    (w2_st, w2_hi, w2_lo, b1a, b1g, lng, lnb, b2t, hh, xr, stt, mv, ve, rstd, hn, hf, thi, tlo, gl, af,
     ahi, alo, xb, x2, pT, pH, pO) = F.tensors
    w1_st, w1_hi, w1_lo = W.weights
    S = F.sems
    g0 = layer * NS

    def steps(e, step):
        with e.Fori(0, NS // 2 - 2) as it:
            step(it * 2 + 1, 1, it)
            step(it * 2 + 2, 0, it + 1)
        step(NS - 3, 1, NS // 2 - 2)
        step(NS - 2, 0, NS // 2 - 1)
        step(NS - 1, 1, NS // 2 - 1)
        step(NS, 0, NS // 2)

    def within(s, n):
        return None if isinstance(s, int) and s + n >= NS else s + n

    with nc.Block() as block:
        @block.sync
        def _(sp):
            def load(dst, src, columns=False):
                sp.dma_start(dst, src, allow_slow_non_contiguous=columns).then_inc(S["w_loaded"], 16)

            load(w1_st[:, :, 0:HA], w1[layer][:, 0:HA].rearrange("(k p) n -> p k n", p=P))
            load(w1_st[:, :, HA:HA + HID], w1[layer][:, HID:2 * HID].rearrange("(k p) n -> p k n", p=P))
            load(lng[:, :], ln_g[layer].rearrange("(k p) -> p k", p=P), True)
            load(lnb[:, :], ln_b[layer].rearrange("(k p) -> p k", p=P), True)
            load(b2t[:, :], b2[layer][None, :].broadcast_to([P, D]))
            load(b1a[:, :], b1[layer][0:HA].rearrange("(c p) -> p c", p=P), True)
            sp.wait_ge(S["cleared"], ONE + 3 * layer + 3)
            load(w2_st[:, 0:HC - 1], w2[layer][0:(HC - 1) * P].rearrange("(c p) n -> p c n", p=P))
            load(w2_st[0:TAIL, HC - 1], w2[layer][(HC - 1) * P:HID])
            load(b1g[:, 0:HC - 1], b1[layer][HID:HID + (HC - 1) * P].rearrange("(c p) -> p c", p=P), True)
            load(b1g[0:TAIL, HC - 1:HC], b1[layer][HID + (HC - 1) * P:2 * HID].rearrange("(p c) -> p c", c=1), True)

            def row(stage, s):
                return stage * ST_ROWS + s * N + s * SUP // TPB + 1

            def load_h(s, j):
                r0 = row(2 * layer + 1, s)
                sp.dma_start(hh[:, j, :, 0:P], X[bass.ds(r0, N), 0:P].rearrange("(n p) d -> p n d", p=P))\
                  .then_inc(S["h_loaded"][j], 16)
                sp.dma_start(hh[:, j, :, P:D], X[bass.ds(r0 - 1, N), P:D].rearrange("(n p) d -> p n d", p=P))\
                  .then_inc(S["h_loaded"][j], 16)

            def load_x(s, j):
                sp.dma_start(xr[:, j], X[bass.ds(row(2 * layer + 1, s), N), :].rearrange("(n p) d -> p n d", p=P))\
                  .then_inc(S["x_loaded"][j], 16)

            def store(s, j):
                sp.wait_ge(S["x2_ready"], ONE + 2 + SUP * (g0 + s + 1))
                sp.dma_start(X[bass.ds(row(2 * layer + 2, s), N), :].rearrange("(n p) d -> p n d", p=P), x2[:, j])\
                  .then_inc(S["x2_stored"][j], 16)

            load_h(0, 0)
            load_h(1, 1)
            load_x(0, 0)
            load_x(1, 1)
            sp.wait_ge(S["hn_ready"], ONE + g0 + 1)
            load_h(2, 0)

            def step(s, j, it):
                if within(s, 2) is not None:
                    sp.wait_ge(S["hn_ready"], ONE + g0 + s + 1)
                    load_h(s + 2, j)
                store(s - 1, 1 - j)
                if within(s, 1) is not None:
                    sp.wait_ge(S["xb_ready"], ONE + g0 + s)
                    load_x(s + 1, 1 - j)

            steps(sp, step)
            for j in range(2):
                sp.wait_ge(S["x2_stored"][j], ONE + (layer + 1) * (NS // 2) * 16)
            sp.sem_inc(K.passed, 1)

        @block.gpsimd
        def _(pool):
            pool.memset(w1_st[:, :, HA + HID:2 * HA], 0.0).then_inc(S["cleared"], 1)
            pool.memset(w2_st[:, HC - 1], 0.0).then_inc(S["cleared"], 1)
            pool.memset(b1g[:, :], 0.0).then_inc(S["cleared"], 1)

            def rstd_of(s, j):
                pool.wait_ge(S["mv_ready"], ONE + (g0 + s + 1) * SUP)
                pool.sem_inc(K.passed, 1)
                pool.tensor_scalar(ve[:, j], mv[:, j, :, 1], 1e-5, None, ALU.add).then_inc(S["ve_ready"], 1)
                pool.wait_ge(S["ve_ready"], ONE + g0 + s + 1)
                pool.tensor_tensor(rstd[:, j], ve[:, j], K.mhalf[:, 0:SUP], ALU.pow).then_inc(S["rstd_ready"], 1)

            def add_b2(s, j, it):
                pool.wait_ge(S["x_loaded"][j], ONE + (layer * (NS // 2) + it + 1) * 16)
                pool.wait_ge(S["x2_ready"], ONE + 2 + SUP * (g0 + s))
                pool.tensor_tensor(xb[:, j], xr[:, j], b2t[:, None, :].broadcast_to([P, SUP, D]), ALU.add)\
                    .then_inc(S["xb_ready"], 1)

            def split(s, j, ch):
                u = (g0 + s) * HC + ch
                pool.wait_ge(S["act_ready"], ONE + 2 + u + 1)
                pool.sem_inc(K.passed, 1)
                pool.tensor_scalar(ahi[:, j, ch], af[:, ch % 2], 1.0, None, ALU.mult).then_inc(S["a_hi"], 1)
                pool.wait_ge(S["a_hi"], ONE + u + 1)
                pool.tensor_tensor(alo[:, j, ch], af[:, ch % 2], ahi[:, j, ch].bitcast(F32), ALU.subtract)\
                    .then_inc(S["a_lo"], 1)

            pool.wait_ge(S["w_split"], ONE + 2 * layer + 2)
            rstd_of(0, 0)
            rstd_of(1, 1)

            def body(s, j, it):
                for ch in range(HC):
                    split(s, j, ch)
                    if ch == 1 and within(s, 2) is not None:
                        rstd_of(s + 2, j)

            body(0, 0, 0)

            def step(s, j, it):
                if within(s, 0) is not None:
                    body(s, j, it)

            def whole(s, j, it):
                add_b2(s - 1, 1 - j, it - 1 + j)
                step(s, j, it)

            steps(pool, whole)

        @block.scalar
        def _(act):
            act.wait_ge(S["w_loaded"], ONE + (layer + 1) * 10 * 16)
            act.wait_ge(S["cleared"], ONE + 3 * layer + 3)
            act.activation(w1_hi[:, :, :], w1_st[:, :, :], ACT.Copy).then_inc(S["w_hi"], 1)
            act.activation(w2_hi[:, :, :], w2_st[:, :, :], ACT.Copy).then_inc(S["w_hi"], 1)

            def turned(s, j):
                act.wait_ge(S["t_ready"], ONE + g0 + s + 1)
                act.wait_ge(S["t_lo"], ONE + g0 + s)
                for k in range(KD):
                    ins = act.activation(hf[:, k], pT[:, k], ACT.Identity, bias=lnb[:, k:k + 1], scale=lng[:, k:k + 1])
                    ins.then_inc(S["hf_ready"], 1)
                act.wait_ge(S["hf_ready"], ONE + KD * (g0 + s + 1))
                act.activation(thi[:, j], hf[:, :, :], ACT.Copy).then_inc(S["t_hi"], 1)

            def gelus(s, j):
                for ch in range(HC):
                    u = (g0 + s) * HC + ch
                    act.wait_ge(S["g_ready"], ONE + u + 1)
                    act.wait_ge(S["act_ready"], ONE + u + 1)
                    act.activation(gl[:, ch % 2], pH[:, ch % 2, 1], ACT.Gelu, bias=b1g[:, ch:ch + 1])\
                       .then_inc(S["gelu_done"], 1)

            turned(0, 0)
            turned(1, 1)
            gelus(0, 0)

            def step(s, j, it):
                if within(s, 1) is not None:
                    turned(s + 1, 1 - j)
                if within(s, 0) is not None:
                    gelus(s, j)

            steps(act, step)

        @block.vector
        def _(dve):
            dve.wait_ge(S["w_hi"], ONE + 2 * layer + 2)
            dve.tensor_tensor(w1_lo[:, :, :], w1_st[:, :, :], w1_hi[:, :, :].bitcast(F32), ALU.subtract)\
               .then_inc(S["w_split"], 1)
            dve.tensor_tensor(w2_lo[:, :, :], w2_st[:, :, :], w2_hi[:, :, :].bitcast(F32), ALU.subtract)\
               .then_inc(S["w_split"], 1)

            def normalise(s, j, it):
                dve.wait_ge(S["h_loaded"][j], ONE + (layer * (NS // 2) + it + 1) * 32)
                for n in range(SUP):
                    dve.bn_stats(stt[:, j, n], hh[:, j, n]).then_inc(S["stats"], 1)
                dve.wait_ge(S["stats"], ONE + (g0 + s) * SUP + SUP)
                dve.sem_inc(K.passed, 1)
                for n in range(SUP):
                    dve.bn_aggr(mv[:, j, n], stt[:, j, n]).then_inc(S["mv_ready"], 1)
                dve.wait_ge(S["rstd_ready"], ONE + g0 + s + 1)
                for n in range(SUP):
                    ins = dve.tensor_scalar(hn[:, j, n], hh[:, j, n], mv[:, j, n, 0:1], rstd[:, j, n:n + 1],
                                            ALU.subtract, ALU.mult)
                ins.then_inc(S["hn_ready"], 1)

            def lo_of(s, j):
                dve.wait_ge(S["t_hi"], ONE + g0 + s + 1)
                dve.tensor_tensor(tlo[:, j], hf[:, :, :], thi[:, j].bitcast(F32), ALU.subtract).then_inc(S["t_lo"], 1)

            def gated(s, j, ch):
                u = (g0 + s) * HC + ch
                dve.wait_ge(S["gelu_done"], ONE + u + 1)
                dve.wait_ge(S["a_lo"], ONE + u)
                dve.scalar_tensor_tensor(af[:, ch % 2], pH[:, ch % 2, 0], b1a[:, ch:ch + 1], gl[:, ch % 2],
                                         ALU.add, ALU.mult).then_inc(S["act_ready"], 1)

            def residual(s, j, it):
                dve.wait_ge(S["xb_ready"], ONE + g0 + s + 1)
                dve.wait_ge(S["x2_stored"][j], ONE + (layer * (NS // 2) + it) * 16)
                for n in range(SUP):
                    dve.wait_ge(S["o_ready"], ONE + (g0 + s) * SUP + n + 1)
                    dve.tensor_tensor(x2[:, j, n], pO[:, n % 2, 0:D], xb[:, j, n], ALU.add).then_inc(S["x2_ready"], 1)

            def body(s, j, it):
                for ch in range(HC):
                    gated(s, j, ch)
                    if ch == 2 and within(s, 2) is not None:
                        normalise(s + 2, j, it + 1)

            normalise(0, 0, 0)
            normalise(1, 1, 0)
            lo_of(0, 0)
            lo_of(1, 1)
            body(0, 0, 0)

            def step(s, j, it):
                if within(s, 1) is not None:
                    lo_of(s + 1, 1 - j)
                if within(s, 0) is not None:
                    body(s, j, it)
                residual(s - 1, 1 - j, it - 1 + j)

            steps(dve, step)

        @block.tensor
        def _(pe):
            def turn(s, j):
                pe.wait_ge(S["hn_ready"], ONE + g0 + s + 1)
                pe.wait_ge(S["hf_ready"], ONE + KD * (g0 + s))
                for k in range(KD):
                    for n in range(SUP):
                        ins = pe.transpose(pT[:, k, n * P:(n + 1) * P], hn[:, j, n, k * P:(k + 1) * P], K.ident[:, :])
                ins.then_inc(S["t_ready"], 1)

            def up(s, j):
                pe.wait_ge(S["t_lo"], ONE + g0 + s + 1)
                for ch in range(HC):
                    u = (g0 + s) * HC + ch
                    pe.wait_ge(S["act_ready"], ONE + u + 1)
                    for half in range(2):
                        cols = slice(half * HA + ch * P, half * HA + (ch + 1) * P)
                        terms = [(m, t, k) for k in range(KD) for m, t in ((w1_hi, thi), (w1_hi, tlo), (w1_lo, thi))]
                        for i, (m, t, k) in enumerate(terms):
                            ins = pe.matmul(pH[:, ch % 2, half], m[:, k, cols], t[:, j, k], start=i == 0,
                                            stop=i == len(terms) - 1)
                    ins.then_inc(S["g_ready"], 1)

            def down(s, j):
                for n in range(SUP):
                    pe.wait_ge(S["a_lo"], ONE + 1 + (g0 + s) * HC + HC)
                    pe.wait_ge(S["x2_ready"], ONE + (g0 + s) * SUP + n + 1)
                    ts = slice(n * P, (n + 1) * P)
                    terms = [(t, m, ch) for ch in range(HC) for t, m in ((ahi, w2_hi), (ahi, w2_lo), (alo, w2_hi))]
                    for i, (t, m, ch) in enumerate(terms):
                        ins = pe.matmul(pO[:, n % 2, 0:D], t[:, j, ch, ts], m[:, ch], start=i == 0,
                                        stop=i == len(terms) - 1)
                    ins.then_inc(S["o_ready"], 1)

            pe.wait_ge(S["w_split"], ONE + 2 * layer + 2)
            turn(0, 0)
            turn(1, 1)
            up(0, 0)

            def step(s, j, it):
                if within(s, 1) is not None:
                    turn(s + 1, 1 - j)
                if within(s, 0) is not None:
                    up(s, j)
                down(s - 1, 1 - j)

            steps(pe, step)



def phase_output(nc, K, AO, X, x, wo, out):
    with ExitStack() as c:
        sb = lambda n, s, d: c.enter_context(nc.sbuf_tensor(n, s, d))
        ps = lambda n, s, d: c.enter_context(nc.psum_tensor(n, s, d))
        mine = []

        def sem(name):
            mine.append(c.enter_context(nc.semaphore(name)))
            return mine[-1]

        wst = sb("p3_wst", [P, KD, D], F32)
        whi = sb("p3_whi", [P, KD, D], F32R)
        wlo = sb("p3_wlo", [P, KD, D], F32R)
        a = sb("p3_a", [P, 2, SUP, D], F32)
        f = sb("p3_f", [P, 2, SUP, D], F32)
        xi = sb("p3_x", [P, 2, SUP, D], F32)
        thi = sb("p3_thi", [P, 2, KD, SUP * P], F32R)
        tlo = sb("p3_tlo", [P, 2, KD, SUP * P], F32R)
        gate = sb("p3_gate", [P, 2, SUP, D], F32)
        prod = sb("p3_prod", [P, 2, SUP, D], F32)
        res = sb("p3_res", [P, 2, SUP, D], F32)
        pT = ps("p3_pT", [P, KD, 512], F32)
        pO = ps("p3_pO", [P, 2, 2, D], F32)
        w_loaded, w_hi, w_split = sem("p3_w_loaded"), sem("p3_w_hi"), sem("p3_w_split")
        a_loaded = [sem(f"p3_a_loaded{i}") for i in range(2)]
        f_loaded = [sem(f"p3_f_loaded{i}") for i in range(2)]
        stored = [sem(f"p3_stored{i}") for i in range(2)]
        t_ready, t_hi, t_lo = sem("p3_t_ready"), sem("p3_t_hi"), sem("p3_t_lo")
        o_ready, prod_ready, gate_ready, res_ready = (
            sem("p3_o_ready"), sem("p3_prod_ready"), sem("p3_gate_ready"), sem("p3_res_ready"))
        tiles = lambda d: d.rearrange("(s n p) d -> s p n d", n=SUP, p=P)
        block = c.enter_context(nc.Block())

        def steps(e, step):
            with e.Fori(0, SUPERS // 2 - 1) as it:
                for j in range(2):
                    step(it * 2 + j, j, it, True)
            step(SUPERS - 2, 0, SUPERS // 2 - 1, True)
            step(SUPERS - 1, 1, SUPERS // 2 - 1, False)

        @block.sync
        def _(sp):
            sp.dma_start(wst[:, :, :], wo.rearrange("(k p) n -> p k n", p=P)).then_inc(w_loaded, 16)

            def load(s, j):
                sp.dma_start(a[:, j], tiles(AO)[s]).then_inc(a_loaded[j], 16)
                r0 = 2 * LAYERS * ST_ROWS + s * SUP * P + s // 2 + 1
                sp.dma_start(f[:, j], X[bass.ds(r0, SUP * P), :].rearrange("(n p) d -> p n d", p=P))\
                  .then_inc(f_loaded[j], 16)
                sp.dma_start(xi[:, j], tiles(x)[s]).then_inc(f_loaded[j], 16)

            load(0, 0)
            load(1, 1)

            def step(s, j, it, more):
                sp.wait_ge(res_ready, ONE + s + 1)
                sp.dma_start(tiles(out)[s], res[:, j]).then_inc(stored[j], 16)
                if not (isinstance(s, int) and s + 2 >= SUPERS):
                    load(s + 2, j)

            steps(sp, step)
            for j in range(2):
                sp.wait_ge(stored[j], ONE + 16 * SUPERS // 2)

        @block.scalar
        def _(act):
            act.wait_ge(w_loaded, ONE + 16)
            act.activation(whi[:, :, :], wst[:, :, :], ACT.Copy).then_inc(w_hi, 1)

            def hi_of(s, j):
                act.wait_ge(t_ready, ONE + s + 1)
                act.activation(thi[:, j], pT[:, :, :], ACT.Copy).then_inc(t_hi, 1)

            hi_of(0, 0)

            def step(s, j, it, more):
                if more:
                    hi_of(s + 1, 1 - j)
                act.wait_ge(f_loaded[j], ONE + (it + 1) * 32)
                act.activation(gate[:, j], f[:, j], ACT.Silu).then_inc(gate_ready, 1)

            steps(act, step)

        @block.vector
        def _(dve):
            start_at_one(dve, mine)
            dve.wait_ge(w_hi, ONE + 1)
            dve.tensor_tensor(wlo[:, :, :], wst[:, :, :], whi[:, :, :].bitcast(F32), ALU.subtract).then_inc(w_split, 1)

            def lo_of(s, j):
                dve.wait_ge(t_hi, ONE + s + 1)
                dve.tensor_tensor(tlo[:, j], pT[:, :, :], thi[:, j].bitcast(F32), ALU.subtract).then_inc(t_lo, 1)

            lo_of(0, 0)
            dve.sem_inc(prod_ready, 2)

            def step(s, j, it, more):
                if more:
                    lo_of(s + 1, 1 - j)
                dve.wait_ge(gate_ready, ONE + s + 1)
                for v in range(2):
                    dve.wait_ge(o_ready, ONE + 2 * s + v + 1)
                    dve.tensor_tensor(prod[:, j, 2 * v:2 * v + 2], pO[:, v], gate[:, j, 2 * v:2 * v + 2],
                                      ALU.mult).then_inc(prod_ready, 1)
                dve.wait_ge(prod_ready, ONE + 2 + 2 * s + 2)
                dve.wait_ge(stored[j], ONE + it * 16)
                dve.tensor_tensor(res[:, j], prod[:, j], xi[:, j], ALU.add).then_inc(res_ready, 1)

            steps(dve, step)

        @block.tensor
        def _(pe):
            def turn(s, j, it):
                pe.wait_ge(a_loaded[j], ONE + (it + 1) * 16)
                pe.wait_ge(t_lo, ONE + s)
                for k in range(KD):
                    for n in range(SUP):
                        ins = pe.transpose(pT[:, k, n * P:(n + 1) * P], a[:, j, n, k * P:(k + 1) * P], K.ident[:, :])
                ins.then_inc(t_ready, 1)

            pe.wait_ge(w_split, ONE + 1)
            turn(0, 0, 0)

            def step(s, j, it, more):
                if more:
                    turn(s + 1, 1 - j, it + j)
                pe.wait_ge(t_lo, ONE + s + 1)
                for n in range(SUP):
                    v, o = n // 2, n % 2
                    if o == 0:
                        pe.wait_ge(prod_ready, ONE + 2 * s + v + 1)
                    ts = slice(n * P, (n + 1) * P)
                    terms = [(t, w, k) for k in range(KD) for t, w in ((thi, whi), (thi, wlo), (tlo, whi))]
                    for i, (t, w, k) in enumerate(terms):
                        ins = pe.matmul(pO[:, v, o], t[:, j, k, ts], w[:, k], start=i == 0, stop=i == len(terms) - 1)
                    if o == 1:
                        ins.then_inc(o_ready, 1)

            steps(pe, step)


def semaphores(c, nc, prefix, names, rings):
    sems = {n: c.enter_context(nc.semaphore(prefix + n)) for n in names}
    sems.update({n: [c.enter_context(nc.semaphore(f"{prefix}{n}{i}")) for i in range(k)] for n, k in rings.items()})
    return sems


def start_at_one(e, sems):
    for s in sems:
        for x in (s if isinstance(s, list) else [s]):
            e.sem_inc(x, ONE)


class Named:
    pass


def window_tensors(nc, c, W):
    sb = lambda n, s, d: c.enter_context(nc.sbuf_tensor("w_" + n, s, d))
    ps = lambda n, s, d: c.enter_context(nc.psum_tensor("w_" + n, s, d))
    W.tensors = (
        sb("wo_st", [P, KI, D], F32), sb("wo_hi", [P, KI, D], F32R), sb("wo_lo", [P, KI, D], F32R),
        sb("scales", [P, 4, LD], F32), sb("tab", [P, TPB, 4, LD], F32),
        sb("xt", [P, 4, D], F32), sb("hs", [P, 4, P], F32),
        sb("thi", [P, 2, KD, P], F32R), sb("tlo", [P, 2, KD, P], F32R),
        sb("qk", [P, 2, 2 * INNER], F32), sb("sq", [P, 2 * INNER], F32),
        sb("ss", [P, 2, 2 * LH], F32), sb("ssc", [P, 2 * LH], F32), sb("rs", [P, 2, 2 * LH], F32),
        sb("tc", [P, 2 * INNER], F32), sb("tsn", [P, 2 * INNER], F32), sb("rr", [P, 2 * INNER], F32),
        sb("qkn", [P, 2 * INNER], F32),
        sb("v", [P, 4, INNER], F32), sb("kt", [P, KI, 2, P], F32), sb("qz", [P, LH, P], F32),
        sb("nmax", [P, LH], F32), sb("sums", [P, LH], F32), sb("rsum", [P, LH], F32),
        sb("pe", [P, LH, 2 * P], F32), sb("pn", [P, LH, 2 * P], F32), sb("pt", [P, 4, 512], F32),
        sb("oth", [P, INNER], F32R), sb("otl", [P, INNER], F32R), sb("x1", [P, 2, D], F32),
        ps("pX", [P, 4, 512], F32), ps("pS", [P, 4, 2, 2 * P], F32))


def feed_tensors(nc, c, F):
    sb = lambda n, s, d: c.enter_context(nc.sbuf_tensor("f_" + n, s, d))
    ps = lambda n, s, d: c.enter_context(nc.psum_tensor("f_" + n, s, d))
    N = SUP * P
    F.tensors = (
        sb("w2_st", [P, HC, D], F32), sb("w2_hi", [P, HC, D], F32R), sb("w2_lo", [P, HC, D], F32R),
        sb("b1a", [P, HC], F32), sb("b1g", [P, HC], F32), sb("lng", [P, KD], F32), sb("lnb", [P, KD], F32),
        sb("b2t", [P, D], F32), sb("hh", [P, 2, SUP, D], F32), sb("xr", [P, 2, SUP, D], F32),
        sb("stt", [P, 2, SUP, 6], F32), sb("mv", [P, 2, SUP, 2], F32), sb("ve", [P, 2, SUP], F32),
        sb("rstd", [P, 2, SUP], F32), sb("hn", [P, 2, SUP, D], F32), sb("hf", [P, KD, N], F32),
        sb("thi", [P, 2, KD, N], F32R), sb("tlo", [P, 2, KD, N], F32R), sb("gl", [P, 2, N], F32),
        sb("af", [P, 2, N], F32), sb("ahi", [P, 2, HC, N], F32R), sb("alo", [P, 2, HC, N], F32R),
        sb("xb", [P, 2, SUP, D], F32), sb("x2", [P, 2, SUP, D], F32),
        ps("pT", [P, KD, N], F32), ps("pH", [P, 2, 2, N], F32), ps("pO", [P, 2, 512], F32))


def program(nc, x, wqk, wv, woc, wqkv, wo, q_scale, k_scale, ln_g, ln_b, w1, b1, w2, b2, tables, out):
    with ExitStack() as c:
        sb = lambda n, s, d: c.enter_context(nc.sbuf_tensor(n, s, d))
        X = nc.dram_tensor("X", [(2 * LAYERS + 1) * ST_ROWS, D], F32, kind="Internal").ap()
        QKP = nc.dram_tensor("QKP", [BATCH * CG, P, 3, SEQ], BF16, kind="Internal").ap()
        VA = nc.dram_tensor("VA", [TOK, CH * VW], F32, kind="Internal").ap()
        AO = nc.dram_tensor("AO", [TOK, D], F32, kind="Internal").ap()

        K = Named()
        K.passed = c.enter_context(nc.semaphore("passed"))
        K.ident = sb("ident", [P, P], F32)
        K.identb = sb("identb", [P, P], BF16)
        K.mhalf = sb("mhalf", [P, 2 * LH], F32)
        K.zeros = sb("zeros", [(2 * LAYERS + 1) * BATCH, D], F32)
        K.masks = sb("masks", [P, 3, 4 * P], BF16)
        K.base = sb("base", [P, TPB, 4, LD], F32)
        WS = semaphores(c, nc, "w_", (
            "w_loaded", "w_hi", "w_split", "cleared", "tab_ready", "x1_ready", "ss_ready", "k_copied", "sq_ready",
            "added", "ts_ready", "ssc_ready", "rs_ready", "rsum_ready", "pn_ready", "t_ready", "t_hi", "t_lo",
            "q_ready", "k_ready", "v_ready", "q_copied", "v_copied", "max_ready", "exp_done", "pt_ready",
            "pt_even", "pt_odd", "kt_ready", "kt_copied", "qt_ready", "qt_copied", "ot_ready", "ot_hi", "ot_lo",
            "tc_ready", "qkn_ready", "s_ready", "wo_ready"), {"x_loaded": 4, "x1_stored": 2})
        FS = semaphores(c, nc, "f_", (
            "w_loaded", "w_hi", "w_split", "cleared", "x2_ready", "hn_ready", "xb_ready", "mv_ready", "ve_ready",
            "rstd_ready", "act_ready", "a_hi", "a_lo", "t_ready", "t_hi", "t_lo", "hf_ready", "g_ready",
            "gelu_done", "stats", "o_ready"), {"h_loaded": 2, "x_loaded": 2, "x2_stored": 2})
        made = c.enter_context(nc.semaphore("made"))
        zeroed = c.enter_context(nc.semaphore("zeroed"))
        with nc.Block() as block:
            @block.gpsimd
            def _(pool):
                pool.memset(K.mhalf[:, :], -0.5)
                pool.memset(K.zeros[:, :], 0.0).then_inc(made, 1)
                pool.wait_ge(made, 1)
                pool.memset(K.ident[:, :], 0.0).then_inc(made, 1)
                pool.memset(K.identb[:, :], 0.0).then_inc(made, 1)
                pool.memset(K.masks[:, :, :], 0.0).then_inc(made, 1)
                pool.wait_ge(made, 4)
                for t in (K.ident, K.identb):
                    pool.affine_select(out=t[:, :], in_=t[:, :], compare_op=ALU.not_equal, fill=1.0,
                                       base=0, pattern=[[-1, P]], channel_multiplier=1).then_inc(made, 1)
                m = K.masks[:, :, :].rearrange("p m (h s t) -> p m h s t", h=2, s=2)
                for kind in range(3):
                    own = kind // 2
                    pool.affine_select(out=m[:, kind, :, own], in_=m[:, kind, :, own], compare_op=ALU.is_ge, fill=NEG,
                                       base=0, pattern=[[0, 2], [-1, P]], channel_multiplier=1).then_inc(made, 1)
                    prev = m[:, kind, :, 1 - own]
                    if kind:
                        pool.affine_select(out=prev, in_=prev, compare_op=ALU.is_ge, fill=NEG,
                                           base=0, pattern=[[0, 2], [1, P]], channel_multiplier=-1).then_inc(made, 1)
                    else:
                        pool.memset(prev, NEG).then_inc(made, 1)

            @block.vector
            def _(dve):
                start_at_one(dve, WS.values())
                start_at_one(dve, FS.values())
                for sem, n in ((WS["kt_copied"], 1), (WS["exp_done"], 2), (WS["x1_ready"], 2), (WS["ot_lo"], 2), (WS["qt_copied"], 1),
                               (FS["act_ready"], 2), (FS["x2_ready"], 2), (FS["a_lo"], 1)):
                    dve.sem_inc(sem, n)

            @block.sync
            def _(sp):
                sp.dma_start(K.base[:, :, :, :], tables).then_inc(zeroed, 16)
                sp.wait_ge(made, 1)
                sp.dma_start(X.rearrange("(g r) d -> g r d", r=SEQ + 1)[:, 0, :], K.zeros[:, :]).then_inc(zeroed, 16)
                sp.wait_ge(zeroed, 32)
        phase_project(nc, K, x, X, QKP, VA, wqk, wv)
        phase_causal(nc, K, QKP, VA, AO)
        with ExitStack() as c2:
            sb2 = lambda n, s, d: c2.enter_context(nc.sbuf_tensor(n, s, d))
            weights = (sb2("big_st", [P, KD, 2 * HC * P], F32), sb2("big_hi", [P, KD, 2 * HC * P], F32R),
                       sb2("big_lo", [P, KD, 2 * HC * P], F32R))
            W, F = Named(), Named()
            W.weights, W.sems, F.sems = weights, WS, FS
            with nc.Fori(0, LAYERS) as layer:
                with ExitStack() as cw:
                    window_tensors(nc, cw, W)
                    phase_window(nc, K, W, layer, X, wqkv, wo, q_scale, k_scale)
                with ExitStack() as cf:
                    feed_tensors(nc, cf, F)
                    phase_feed(nc, K, W, F, layer, X, ln_g, ln_b, w1, b1, w2, b2)
        phase_output(nc, K, AO, X, x, woc, out)


def rotary_tables():
    f = np.float32
    half = np.arange(0, LD, 2, dtype=f)
    inv = (f(1) / f(10000) ** (half / f(LD))).astype(f)
    t = np.arange(SEQ, dtype=f)
    freqs = t[:, None] * inv[None, :]
    base = ((half + f(0.4 * LD)) / f(1.4 * LD)).astype(f)
    scale = base[None, :] ** ((t - SEQ // 2) / f(P // 2))[:, None]
    cos, sin = np.cos(freqs), np.sin(freqs)
    two = lambda a, b: np.concatenate([a, b], axis=-1)
    out = np.stack([two(cos * scale, cos * scale) * f(QK_SCALE), two(-sin * scale, sin * scale) * f(QK_SCALE),
                    two(cos / scale, cos / scale), two(-sin / scale, sin / scale)], axis=1)
    return np.ascontiguousarray(out.reshape(TPB, P, 4, LD).transpose(1, 0, 2, 3).astype(f))


def kernel(**inputs):
    import concourse.bacc as bacc
    from concourse.bass_utils import run_bass_kernel_spmd

    g = {k: np.ascontiguousarray(v) for k, v in inputs.items()}
    wq, wk = (g[f"L0_attn_W_{n}"].T.reshape(D, CG, GH * CD) for n in "qk")
    arrays = {
        "x": g["L0_attn_x"].reshape(TOK, D),
        "wqk": np.ascontiguousarray(np.stack([wq, wk], axis=2).reshape(D, 2 * D)),
        "wv": np.ascontiguousarray(g["L0_attn_W_v"].T),
        "woc": np.ascontiguousarray(g["L0_attn_W_o"].T),
        **{n: g["L0_ffn_" + n] for n in ("wqkv", "wo", "q_scale", "k_scale", "ln_g", "ln_b", "w1", "b1", "w2", "b2")},
        "tables": rotary_tables(),
    }
    nc = bacc.Bacc("TRN2", target_bir_lowering=False, num_devices=1)
    args = {n: nc.dram_tensor(n, a.shape, mybir.dt.from_np(a.dtype), kind="ExternalInput").ap()
            for n, a in arrays.items()}
    out = nc.dram_tensor("out", (TOK, D), F32, kind="ExternalOutput").ap()
    program(nc, out=out, **args)
    r = run_bass_kernel_spmd(nc, [arrays], core_ids=[0])
    return r.results[0]["out"].reshape(BATCH, SEQ, D)
```

```python
import numpy as np
import concourse.bass as bass
from concourse import mybir
from contextlib import ExitStack

F32 = mybir.dt.float32
F32R = mybir.dt.float32r
BF16 = mybir.dt.bfloat16
ALU = mybir.AluOpType
ACT = mybir.ActivationFunctionType
AX = mybir.AxisListType

P = 128
D = 256
KD = D // P
BATCH, SEQ = 4, 1024
TOK = BATCH * SEQ
TILES = TOK // P
TPB = SEQ // P
SUP = 4
SUPERS = TILES // SUP
ST_ROWS = BATCH * (SEQ + 1)
CH, CD = 16, 16
GH = 4
CG = CH // GH
CS = CD ** -0.5
VW = 32
PAIRS = [(0, 0), (0, 1), (0, 2), (1, 0), (1, 1), (2, 0)]
SHIFT_ROW = len(PAIRS) * CD
SROWS = SHIFT_ROW + 2
SLOTS = 3
LOADS = 2 * len(PAIRS) + 1
LAYERS = 2
LH, LD = 8, 64
INNER = LH * LD
KI = INNER // P
HID = 682
HC = 6
QK_SCALE = 8.0
NEG = -1e30
ONE = 1
BIG = 3e38


def stage_row(stage, tile):
    return stage * ST_ROWS + tile * P + tile // TPB + 1


def stack_transfers(K, QKP, VA, n, u):
    qs, ks, va, _ = K.stacks
    parts = QKP[n].rearrange("(z h d) c s -> z c d h s", z=2, h=GH)
    out = []
    for r, (a, k) in enumerate(PAIRS):
        rows = slice(r * CD, (r + 1) * CD)
        out += [(qs[rows, u], parts[0, a]), (ks[rows, u], parts[1, k])]
    va_t = VA.rearrange("(b t p) (g c) -> b g p t c", b=BATCH, p=P, g=CG)
    return out + [(va[:, u], va_t[n // CG, n % CG])]


def phase_project(nc, K, x, X, QKP, VA, wqk, wv):
    with ExitStack() as c:
        sb = lambda n, s, d: c.enter_context(nc.sbuf_tensor(n, s, d))
        ps = lambda n, s, d: c.enter_context(nc.psum_tensor(n, s, d))
        mine = []

        def sem(name):
            mine.append(c.enter_context(nc.semaphore(name)))
            return mine[-1]

        wst = sb("p1_wst", [P, KD, 768], F32)
        whi = sb("p1_whi", [P, KD, 768], F32R)
        wlo = sb("p1_wlo", [P, KD, 768], F32R)
        xin = sb("p1_xin", [P, 2, SUP, D], F32)
        stt = sb("p1_stt", [P, 2, SUP, 6], F32)
        mv = sb("p1_mv", [P, 2, SUP, 2], F32)
        ve = sb("p1_ve", [P, 2, SUP], F32)
        rstd = sb("p1_rstd", [P, 2, SUP], F32)
        xn = sb("p1_xn", [P, 2, SUP, D], F32)
        thi = sb("p1_thi", [P, 2, KD, SUP * P], F32R)
        tlo = sb("p1_tlo", [P, 2, KD, SUP * P], F32R)
        parts = sb("p1_parts", [P, CG, 3, SUP * P], BF16)
        rest = sb("p1_rest", [P, CG, SUP * P], F32)
        vaug = sb("p1_vaug", [P, 2, SUP, CH, VW], F32)
        pT = ps("p1_pT", [P, KD, 512], F32)
        pQ = ps("p1_pQ", [P, 4, 512], F32)
        pV = ps("p1_pV", [P, 2, 2, D], F32)

        w_loaded, w_hi, w_split, masked = sem("p1_w_loaded"), sem("p1_w_hi"), sem("p1_w_split"), sem("p1_masked")
        x_loaded = [sem(f"p1_x_loaded{i}") for i in range(2)]
        stats = sem("p1_stats")
        mv_ready, ve_ready, rstd_ready = sem("p1_mv_ready"), sem("p1_ve_ready"), sem("p1_rstd_ready")
        xn_ready = sem("p1_xn_ready")
        xn_stored = [sem(f"p1_xn_stored{i}") for i in range(2)]
        t_ready, t_hi, t_lo = sem("p1_t_ready"), sem("p1_t_hi"), sem("p1_t_lo")
        q_ready, part0, rest_ready, part1, part2 = (
            sem("p1_q_ready"), sem("p1_part0"), sem("p1_rest_ready"), sem("p1_part1"), sem("p1_part2"))
        part_stored = [sem(f"p1_part_stored{i}") for i in range(CG)]
        v_ready, v_copied, v_preset = sem("p1_v_ready"), sem("p1_v_copied"), sem("p1_v_preset")
        v_stored = [sem(f"p1_v_stored{i}") for i in range(2)]

        x_t = x.rearrange("(s n p) d -> s p n d", n=SUP, p=P)
        va_t = VA.rearrange("(s n p) c -> s p n c", n=SUP, p=P)
        block = c.enter_context(nc.Block())

        def steps(e, first, step):
            first()
            with e.Fori(0, SUPERS // 2 - 1) as it:
                for j in range(2):
                    step(it * 2 + j, j, it, False)
            step(SUPERS - 2, 0, SUPERS // 2 - 1, False)
            step(SUPERS - 1, 1, SUPERS // 2 - 1, True)

        @block.sync
        def _(sp):
            sp.dma_start(xin[:, 0], x_t[0]).then_inc(x_loaded[0], 16)
            sp.dma_start(wst[:, :, 0:512], wqk.rearrange("(k p) n -> p k n", p=P)).then_inc(w_loaded, 16)
            sp.dma_start(wst[:, :, 512:768], wv.rearrange("(k p) n -> p k n", p=P)).then_inc(w_loaded, 16)
            sp.dma_start(xin[:, 1], x_t[1]).then_inc(x_loaded[1], 16)

            def store_xn(s, j, it):
                sp.wait_ge(xn_ready, ONE + s + 1)
                row = s * SUP * P + it + 1
                sp.dma_start(X[bass.ds(row, SUP * P), :].rearrange("(n p) d -> p n d", p=P),
                             xn[:, j]).then_inc(xn_stored[j], 16)

            def rest_of(s, j, it):
                for g in range(CG):
                    sp.wait_ge(part2, ONE + CG + s * CG + g + 1)
                    sp.dma_start(QKP[it * CG + g, :, :, j * 512:(j + 1) * 512],
                                 parts[:, g]).then_inc(part_stored[g], 16)
                    if isinstance(s, int) and s == SUPERS - 2:
                        if g == 0:
                            sp.wait_ge(part_stored[0], ONE + 2 * 16)
                            for i in range(2):
                                sp.wait_ge(v_stored[i], ONE + 16)
                        share = -(-LOADS // CG)
                        for transfer in stack_transfers(K, QKP, VA, 0, 0)[g * share:(g + 1) * share]:
                            sp.dma_start(*transfer).then_inc(K.stacks[3][0], 16)
                sp.wait_ge(v_copied, ONE + 2 + s * 2 + 2)
                sp.dma_start(va_t[s], vaug[:, j].rearrange("p n h w -> p n (h w)")).then_inc(v_stored[j], 16)

            def step(s, j, it, final):
                store_xn(s, j, it)
                if not final and not (isinstance(s, int) and s >= SUPERS - 2):
                    sp.dma_start(xin[:, j], x_t[s + 2]).then_inc(x_loaded[j], 16)
                rest_of(s, j, it)

            steps(sp, lambda: None, step)
            for j in range(2):
                sp.wait_ge(xn_stored[j], ONE + 16 * SUPERS // 2)
                sp.wait_ge(v_stored[j], ONE + 16 * SUPERS // 2)
            for g in range(CG):
                sp.wait_ge(part_stored[g], ONE + 16 * SUPERS)
            sp.wait_ge(K.zeroed, 32)

        @block.gpsimd
        def _(pool):
            pool.sem_inc(part2, CG)

            def rstd_of(s, j):
                pool.wait_ge(mv_ready, ONE + (s + 1) * SUP)
                pool.sem_inc(K.passed, 1)
                pool.tensor_scalar(ve[:, j], mv[:, j, :, 1], 1e-5, None, ALU.add).then_inc(ve_ready, 1)
                pool.wait_ge(ve_ready, ONE + s + 1)
                pool.tensor_tensor(rstd[:, j], ve[:, j], K.mhalf[:, 0:SUP], ALU.pow).then_inc(rstd_ready, 1)

            def step(s, j, it, final):
                if not final:
                    rstd_of(s + 1, 1 - j)
                for g in range(CG):
                    pool.wait_ge(part1, ONE + s * CG + g + 1)
                    pool.tensor_tensor(parts[:, g, 2], rest[:, g], parts[:, g, 1],
                                       ALU.subtract).then_inc(part2, 1)

            def first():
                rstd_of(0, 0)
                pool.memset(vaug[:, :, :, :, CD + 1:VW], 0.0).then_inc(v_preset, 1)
                pool.memset(vaug[:, :, :, :, CD:CD + 1], 1.0).then_inc(v_preset, 1)

            steps(pool, first, step)
            pool.memset(K.masks[:, :, :], 0.0).then_inc(masked, 1)
            pool.wait_ge(masked, ONE + 1)
            m = K.masks[:, :, :].rearrange("p m (h s t) -> p m h s t", h=2, s=2)
            for kind in range(3):
                own = kind // 2
                pool.affine_select(out=m[:, kind, :, own], in_=m[:, kind, :, own], compare_op=ALU.is_ge, fill=NEG,
                                   base=0, pattern=[[0, 2], [-1, P]], channel_multiplier=1).then_inc(masked, 1)
                prev = m[:, kind, :, 1 - own]
                if kind:
                    pool.affine_select(out=prev, in_=prev, compare_op=ALU.is_ge, fill=NEG,
                                       base=0, pattern=[[0, 2], [1, P]], channel_multiplier=-1).then_inc(masked, 1)
                else:
                    pool.memset(prev, NEG).then_inc(masked, 1)

        @block.scalar
        def _(act):
            act.wait_ge(w_loaded, ONE + 32)
            act.activation(whi[:, :, :], wst[:, :, :], ACT.Copy).then_inc(w_hi, 1)

            def hi_of(s, j):
                act.wait_ge(t_ready, ONE + s + 1)
                act.activation(thi[:, j], pT[:, :, :], ACT.Copy).then_inc(t_hi, 1)

            def step(s, j, it, final):
                for g in range(CG):
                    u = s * CG + g
                    act.wait_ge(q_ready, ONE + u + 1)
                    act.wait_ge(part_stored[g], ONE + s * 16)
                    act.activation(parts[:, g, 0], pQ[:, g], ACT.Copy).then_inc(part0, 1)
                    act.wait_ge(rest_ready, ONE + CG + u + 1)
                    act.activation(parts[:, g, 1], rest[:, g], ACT.Copy).then_inc(part1, 1)
                    if g == CG - 2 and not final:
                        hi_of(s + 1, 1 - j)

            steps(act, lambda: hi_of(0, 0), step)

        @block.vector
        def _(dve):
            start_at_one(dve, mine + K.stacks[3])
            dve.sem_inc(rest_ready, CG)
            dve.sem_inc(v_copied, 2)

            def moments(s, j, it):
                dve.wait_ge(x_loaded[j], ONE + (it + 1) * 16)
                for n in range(SUP):
                    dve.bn_stats(stt[:, j, n], xin[:, j, n]).then_inc(stats, 1)
                dve.wait_ge(stats, ONE + s * SUP + SUP)
                dve.sem_inc(K.passed, 1)
                for n in range(SUP):
                    dve.bn_aggr(mv[:, j, n], stt[:, j, n]).then_inc(mv_ready, 1)

            def normalise(s, j, it):
                dve.wait_ge(xn_stored[j], ONE + it * 16)
                dve.wait_ge(rstd_ready, ONE + s + 1)
                for n in range(SUP):
                    ins = dve.tensor_scalar(xn[:, j, n], xin[:, j, n], mv[:, j, n, 0:1], rstd[:, j, n:n + 1],
                                            ALU.subtract, ALU.mult)
                ins.then_inc(xn_ready, 1)

            def lo_of(s, j):
                dve.wait_ge(t_hi, ONE + s + 1)
                dve.tensor_tensor(tlo[:, j], pT[:, :, :], thi[:, j].bitcast(F32), ALU.subtract).then_inc(t_lo, 1)

            def first():
                moments(0, 0, 0)
                normalise(0, 0, 0)
                dve.wait_ge(w_hi, ONE + 1)
                dve.tensor_tensor(wlo[:, :, :], wst[:, :, :], whi[:, :, :].bitcast(F32), ALU.subtract).then_inc(w_split, 1)
                lo_of(0, 0)
                dve.wait_ge(v_preset, ONE + 2)

            def step(s, j, it, final):
                if not final:
                    moments(s + 1, 1 - j, it + j)
                for g in range(CG):
                    if g == 1 and not final:
                        normalise(s + 1, 1 - j, it + j)
                    u = s * CG + g
                    dve.wait_ge(part0, ONE + u + 1)
                    dve.wait_ge(part2, ONE + u + 1)
                    dve.tensor_tensor(rest[:, g], pQ[:, g], parts[:, g, 0], ALU.subtract).then_inc(rest_ready, 1)
                    if g == CG - 2 and not final:
                        lo_of(s + 1, 1 - j)
                for v in range(2):
                    dve.wait_ge(v_ready, ONE + s * 2 + v + 1)
                    if v == 0:
                        dve.wait_ge(v_stored[j], ONE + it * 16)
                    dve.tensor_copy(vaug[:, j, 2 * v:2 * v + 2, :, 0:CD],
                                    pV[:, v].rearrange("p n (h w) -> p n h w", w=CD)).then_inc(v_copied, 1)

            steps(dve, first, step)

        @block.tensor
        def _(pe):
            def transposes(s, j):
                pe.wait_ge(xn_ready, ONE + s + 1)
                pe.wait_ge(t_lo, ONE + s)
                for k in range(KD):
                    for n in range(SUP):
                        ins = pe.transpose(pT[:, k, n * P:(n + 1) * P], xn[:, j, n, k * P:(k + 1) * P], K.ident[:, :])
                ins.then_inc(t_ready, 1)

            def first():
                transposes(0, 0)
                pe.wait_ge(w_split, ONE + 1)

            def step(s, j, it, final):
                pe.wait_ge(t_lo, ONE + s + 1)
                for g in range(CG):
                    pe.wait_ge(rest_ready, ONE + s * CG + g + 1)
                    ws = slice(g * P, (g + 1) * P)
                    terms = [(w, t, k) for k in range(KD) for w, t in ((whi, thi), (whi, tlo), (wlo, thi))]
                    for i, (w, t, k) in enumerate(terms):
                        ins = pe.matmul(pQ[:, g], w[:, k, ws], t[:, j, k], start=i == 0, stop=i == len(terms) - 1)
                    ins.then_inc(q_ready, 1)
                    if g == CG - 2 and not final:
                        transposes(s + 1, 1 - j)
                for n in range(SUP):
                    v, o = n // 2, n % 2
                    if o == 0:
                        pe.wait_ge(v_copied, ONE + s * 2 + v + 1)
                    ts = slice(n * P, (n + 1) * P)
                    terms = [(t, w, k) for k in range(KD) for t, w in ((thi, whi), (thi, wlo), (tlo, whi))]
                    for i, (t, w, k) in enumerate(terms):
                        ins = pe.matmul(pV[:, v, o], t[:, j, k, ts], w[:, k, 512:768], start=i == 0, stop=i == len(terms) - 1)
                    if o == 1:
                        ins.then_inc(v_ready, 1)

            steps(pe, first, step)


def phase_causal(nc, K, QKP, VA, AO):
    ITERS = BATCH * CG
    RING = 3
    MAXJOBS = [(h, i, ch) for i in range(TPB - 1, -1, -1) for h in range(GH) for ch in range(1 + i // 4)]
    NJ = len(MAXJOBS)
    PER = [6, 5, 4, 4, 5, 5, 5, 5, 2, 0, 0, 0]
    EARLY = {10: (0, 3), 11: (3, 7)}
    A, B = 2, 3
    NEARLY = max(end for _, end in EARLY.values())
    STEPS = [(0, j) for j in range(TPB // 2)] + [(1, j) for j in range(TPB)]
    NSTEP = len(STEPS)
    SHIFT_STEP = 9
    OUT_STEP = 5
    LATE_STEP = 1
    RJ = NJ + 3
    HALF = SEQ // 2
    LOOPS = (ITERS - 2) // SLOTS

    def plan(started, more):
        at, chunk, index = [], NEARLY, NJ + NEARLY + (not started) - (0 if more else NEARLY)
        for k in range(NSTEP):
            todo = []
            if more == 2:
                todo += [("early", i) for i in range(*EARLY.get(k, (0, 0)))]
            if more:
                for _ in range(PER[k]):
                    todo.append(("max", chunk))
                    chunk += 1
                if k == SHIFT_STEP:
                    todo.append(("shift", 0))
            if k == LATE_STEP and started:
                todo.append(("out", 1))
            if k == OUT_STEP:
                todo.append(("out", 0))
            at.append([(index + i, *t) for i, t in enumerate(todo)])
            index += len(todo)
        return at, index

    def span(k):
        half, j = STEPS[k]
        q0 = max(half * HALF, j * P)
        return q0, (half + 1) * HALF - q0

    with ExitStack() as c:
        sb = lambda n, s, d: c.enter_context(nc.sbuf_tensor(n, s, d))
        ps = lambda n, s, d: c.enter_context(nc.psum_tensor(n, s, d))
        mine = []

        def sem(name):
            mine.append(c.enter_context(nc.semaphore(name)))
            return mine[-1]

        qs, ks, va, loaded = K.stacks
        mask_q = sb("ca_mask_q", [P, P], BF16)
        mask_k = sb("ca_mask_k", [P, P], BF16)
        mx = sb("ca_mx", [P, TPB, GH, 2], F32)
        nm = sb("ca_nm", [P, TPB, GH], F32)
        nms = sb("ca_nms", [P, TPB, 2, GH], BF16)
        shift = sb("ca_shift", [2 * GH, SEQ], BF16)
        pr = sb("ca_pr", [P, 2, 2, 2, 512], F32)
        ot = sb("ca_ot", [P, 2, 512], F32)
        rec = sb("ca_rec", [P, 2, SUP, GH], F32)
        att = sb("ca_att", [P, 2, SUP, GH, CD], F32)
        pS = ps("ca_pS", [P, 2, 2, 512], F32)
        pR = [ps(f"ca_pR{i}", [P, 512], F32) for i in range(RING)]
        pO = ps("ca_pO", [P, 512], F32)

        made, ones = sem("ca_made"), sem("ca_ones")
        shifted = [sem(f"ca_shifted{i}") for i in range(SLOTS)]
        ring_full, ring_free = sem("ca_ring_full"), sem("ca_ring_free")
        min_done, hi_done, split_done = sem("ca_min_done"), sem("ca_hi_done"), sem("ca_split_done")
        s_ready, p_ready, pv_done = sem("ca_s_ready"), sem("ca_p_ready"), sem("ca_pv_done")
        ot_copied, rec_done = sem("ca_ot_copied"), sem("ca_rec_done")
        att_stored = [sem(f"ca_att_stored{i}") for i in range(2)]

        ao_t = AO.rearrange("(b f t p) (g c) -> b f g p t c", b=BATCH, f=2, p=P, g=CG)
        block = c.enter_context(nc.Block())

        def run(e, first, step):
            first()
            step(0, 0, 0, False, 2)
            with e.Fori(0, LOOPS) as it:
                for u in range(1, SLOTS + 1):
                    step(it * SLOTS + u, u % SLOTS, it + u // SLOTS, True, 2)
            for n in range(LOOPS * SLOTS + 1, ITERS):
                step(n, n % SLOTS, n // SLOTS, True, min(ITERS - 1 - n, 2))

        @block.gpsimd
        def _(pool):
            pool.memset(mask_q[:, :], 0.0).then_inc(made, 1)
            pool.memset(mask_k[:, :], 0.0).then_inc(made, 1)
            pool.memset(mx[:, :, :, :], BIG).then_inc(made, 1)
            pool.wait_ge(made, ONE + 3)
            pool.affine_select(out=mask_q[:, :], in_=mask_q[:, :], compare_op=ALU.is_ge, fill=NEG,
                               base=0, pattern=[[-1, P]], channel_multiplier=1).then_inc(made, 1)
            pool.affine_select(out=mask_k[:, :], in_=mask_k[:, :], compare_op=ALU.is_ge, fill=NEG,
                               base=0, pattern=[[1, P]], channel_multiplier=-1).then_inc(made, 1)
            pool.wait_ge(made, ONE + 5)
            for u in range(SLOTS):
                pool.memset(ks[SHIFT_ROW:SROWS, u, :, :], 1.0).then_inc(ones, 1)
                pool.wait_ge(ones, ONE + u + 1)
            for s, n in K.starts:
                pool.sem_inc(s, n)

        @block.sync
        def _(sp):
            def load(n, u):
                for transfer in stack_transfers(K, QKP, VA, n, u):
                    sp.dma_start(*transfer).then_inc(loaded[u], 16)

            def place_shift(u, jobs):
                sp.wait_ge(ring_free, ONE + RING + jobs)
                for part in range(2):
                    sp.dma_start(qs[SHIFT_ROW + part:SHIFT_ROW + part + 1, u, :, :],
                                 shift[part * GH:(part + 1) * GH, :]).then_inc(shifted[u], 16)

            def store(n, half, jobs):
                sp.wait_ge(ring_free, ONE + RING + jobs)
                sp.dma_start(ao_t[n // CG, half, n % CG], att[:, half].rearrange("p t h d -> p t (h d)"))\
                  .then_inc(att_stored[half], 16)

            def first():
                for n in range(1, SLOTS):
                    load(n, n)
                place_shift(0, NJ + NEARLY + 1)

            def step(n, u, it, started, more):
                at, _ = plan(started, more)
                for job, kind, half in sum(at, []):
                    if kind == "out":
                        store(n - half, half, n * RJ + job + 1)
                    elif kind == "shift":
                        place_shift((u + 1) % SLOTS, n * RJ + job + 1)
                    if kind == "out" and half == 1 and not (isinstance(n, int) and n - 1 + SLOTS >= ITERS):
                        load(n - 1 + SLOTS, (u - 1) % SLOTS)

            run(sp, first, step)
            store(ITERS - 1, 1, (ITERS - 1) * RJ + NJ + 3)
            for half in range(2):
                sp.wait_ge(att_stored[half], ONE + ITERS * 16)

        @block.tensor
        def _(pe):
            def ring(job, n):
                pe.wait_ge(ring_free, ONE + n * RJ + job + 1)
                return pR[job % RING]

            def maxima(idx, n, u, job):
                h, i, ch = MAXJOBS[idx]
                k0 = ch * 512
                w = min((i + 1) * P - k0, 512)
                bank = ring(*job)
                diag = k0 + w == (i + 1) * P
                ins = pe.matmul(bank[:, 0:w], qs[0:SHIFT_ROW, u, h, i * P:(i + 1) * P],
                                ks[0:SHIFT_ROW, u, h, k0:k0 + w], start=True, stop=not diag)
                if diag:
                    ins = pe.matmul(bank[:, w - P:w], K.identb[:, :], mask_q[:, :], start=False, stop=True)
                ins.then_inc(ring_full, 1)

            def load_wait(u, it):
                pe.wait_ge(loaded[u % SLOTS], ONE + (it + 1 + u // SLOTS) * LOADS * 16)

            def turn_shift(n, job):
                pe.wait_ge(split_done, ONE + n + 1)
                view = ring(*job)[0:2 * GH, :].bitcast(BF16)
                for i in range(TPB):
                    ins = pe.transpose(view[:, i * P:(i + 1) * P], nms[:, i].rearrange("p a h -> p (a h)"),
                                       K.identb[:, :])
                ins.then_inc(ring_full, 1)

            def scores(n, u, k, pair):
                half, j = STEPS[k]
                q0, w = span(k)
                pe.wait_ge(p_ready, ONE + n * 2 * NSTEP + 2 * k + pair + 1)
                for hh in range(2):
                    h = pair * 2 + hh
                    diag = j * P >= half * HALF
                    ins = pe.matmul(pS[:, pair, hh, 0:w], ks[:, u, h, j * P:(j + 1) * P],
                                    qs[:, u, h, q0:q0 + w], start=True, stop=not diag)
                    if diag:
                        ins = pe.matmul(pS[:, pair, hh, 0:P], K.identb[:, :], mask_k[:, :], start=False, stop=True)
                ins.then_inc(s_ready, 1)

            def weighted(n, u, k):
                half, j = STEPS[k]
                q0, w = span(k)
                o = q0 - half * HALF
                pe.wait_ge(p_ready, ONE + 2 + n * 2 * NSTEP + 2 * k + 2)
                if j == 0:
                    pe.wait_ge(ot_copied, ONE + n * 2 + half)
                last = j == (half + 1) * (TPB // 2) - 1
                for h in range(GH):
                    ins = pe.matmul(pO[h * VW:(h + 1) * VW, o:o + w], va[:, u, j, h * VW:(h + 1) * VW],
                                    pr[:, k % 2, h // 2, h % 2, 0:w], start=j == 0, stop=last)
                ins.then_inc(pv_done, 1)

            def turn_out(n, half, job):
                pe.wait_ge(ot_copied, ONE + n * 2 + half + 1)
                bank = ring(*job)
                for t in range(SUP):
                    ins = pe.transpose(bank[:, t * P:(t + 1) * P], ot[:, half, t * P:(t + 1) * P], K.ident[:, :])
                ins.then_inc(ring_full, 1)

            def first():
                pe.wait_ge(loaded[0], ONE + LOADS * 16)
                for idx in range(NJ):
                    maxima(idx, 0, 0, (idx, 0))
                load_wait(1, 0)
                for idx in range(NEARLY):
                    maxima(idx, 1, 1, (NJ + idx, 0))
                turn_shift(0, (NJ + NEARLY, 0))

            def step(n, u, it, started, more):
                at, _ = plan(started, more)

                def do(jobs):
                    for job, kind, which in jobs:
                        if kind == "max":
                            maxima(which, n + 1, (u + 1) % SLOTS, (job, n))
                        elif kind == "early":
                            if which == 0:
                                load_wait(u + 2, it)
                            maxima(which, n + 2, (u + 2) % SLOTS, (job, n))
                        elif kind == "shift":
                            turn_shift(n + 1, (job, n))
                        else:
                            turn_out(n - which, which, (job, n))

                if not started:
                    pe.wait_ge(ones, ONE + SLOTS)
                pe.wait_ge(shifted[u], ONE + (it + 1) * 2 * 16)
                for k in range(NSTEP):
                    scores(n, u, k, 0)
                    do(at[k][:A])
                    scores(n, u, k, 1)
                    do(at[k][A:B])
                    if k:
                        weighted(n, u, k - 1)
                    elif started:
                        weighted(n - 1, (u - 1) % SLOTS, NSTEP - 1)
                    do(at[k][B:])

            pe.wait_ge(made, ONE + 5)
            run(pe, first, step)
            weighted(ITERS - 1, (ITERS - 1) % SLOTS, NSTEP - 1)
            turn_out(ITERS - 1, 1, (NJ + 2, ITERS - 1))

        @block.scalar
        def _(act):
            def step(n, u, it, started, more):
                for k in range(NSTEP):
                    q0, w = span(k)
                    for pair in range(2):
                        act.wait_ge(s_ready, ONE + n * 2 * NSTEP + 2 * k + pair + 1)
                        act.wait_ge(pv_done, ONE + n * NSTEP + max(k - 1, 0))
                        act.activation(pr[:, k % 2, pair, :, 0:w], pS[:, pair, :, 0:w], ACT.Exp,
                                       scale=CS).then_inc(p_ready, 1)
                    if k == 0 and started:
                        copy_out(n - 1, 1)
                    if k == TPB // 2:
                        copy_out(n, 0)

            def copy_out(n, half):
                act.wait_ge(pv_done, ONE + n * NSTEP + (TPB // 2, NSTEP)[half])
                act.activation(ot[:, half], pO[:, :], ACT.Copy).then_inc(ot_copied, 1)

            act.sem_inc(p_ready, 2)
            run(act, lambda: None, step)
            copy_out(ITERS - 1, 1)

        @block.vector
        def _(dve):
            start_at_one(dve, mine)
            def take_max(idx, job):
                h, i, ch = MAXJOBS[idx]
                w = min((i + 1) * P - ch * 512, 512)
                jb, n = job
                dve.wait_ge(ring_full, ONE + n * RJ + jb + 1)
                dve.tensor_reduce(mx[:, i, h, ch:ch + 1], pR[jb % RING][:, 0:w], AX.X, ALU.max,
                                  negate=True).then_inc(ring_free, 1)

            def split(n, jobs_before):
                dve.wait_ge(ring_free, ONE + RING + jobs_before)
                dve.tensor_tensor(nm[:, :, :], mx[:, :, :, 0], mx[:, :, :, 1], ALU.min).then_inc(min_done, 1)
                dve.wait_ge(min_done, ONE + n + 1)
                dve.tensor_copy(nms[:, :, 0], nm[:, :, :]).then_inc(hi_done, 1)
                dve.wait_ge(hi_done, ONE + n + 1)
                dve.tensor_tensor(nms[:, :, 1], nm[:, :, :], nms[:, :, 0], ALU.subtract).then_inc(split_done, 1)

            def take_shift(job):
                jb, m = job
                dve.wait_ge(ring_full, ONE + m * RJ + jb + 1)
                dve.tensor_copy(shift[:, :], pR[jb % RING][0:2 * GH, :].bitcast(BF16)).then_inc(ring_free, 1)

            def take_out(n, half, job):
                jb, m = job
                dve.wait_ge(ring_full, ONE + m * RJ + jb + 1)
                v = pR[jb % RING][:, :].rearrange("p (t h c) -> p t h c", t=SUP, h=GH)
                dve.reciprocal(rec[:, half], v[:, :, :, CD]).then_inc(rec_done, 1)
                dve.wait_ge(rec_done, ONE + n * 2 + half + 1)
                dve.wait_ge(att_stored[half], ONE + n * 16)
                dve.tensor_tensor(att[:, half], v[:, :, :, 0:CD],
                                  rec[:, half, :, :, None].broadcast_to([P, SUP, GH, CD]),
                                  ALU.mult).then_inc(ring_free, 1)

            def first():
                for idx in range(NJ):
                    take_max(idx, (idx, 0))
                split(0, NJ)
                for idx in range(NEARLY):
                    take_max(idx, (NJ + idx, 0))
                take_shift((NJ + NEARLY, 0))

            def step(n, u, it, started, more):
                at, _ = plan(started, more)
                for job, kind, which in sum(at, []):
                    if kind == "early":
                        take_max(which, (job, n))
                    elif kind == "max":
                        take_max(which, (job, n))
                        if which == NJ - 1:
                            split(n + 1, n * RJ + job + 1)
                    elif kind == "shift":
                        dve.wait_ge(shifted[u], ONE + (it + 1) * 2 * 16)
                        take_shift((job, n))
                    else:
                        take_out(n - which, which, (job, n))

            dve.wait_ge(made, ONE + 5)
            dve.sem_inc(ring_free, RING)
            run(dve, first, step)
            take_out(ITERS - 1, 1, (NJ + 2, ITERS - 1))


def load_h(sp, F, layer, X, s, j):
    r0 = (2 * layer + 1) * ST_ROWS + s * SUP * P + s * SUP // TPB + 1
    for cols, first in ((slice(0, P), r0), (slice(P, D), r0 - 1)):
        sp.dma_start(F.hh[:, j, :, cols], X[bass.ds(first, SUP * P), cols].rearrange("(n p) d -> p n d", p=P))\
          .then_inc(F.sems["h_loaded"][j], 16)


def phase_window(nc, K, W, F, layer, X, wqkv, wo, qk_scales, w1):
    NW = TILES
    (wo_st, wo_hi, wo_lo, scales, tab, xt, hs, thi, tlo, qk, sq, ss, ssc, rs,
     tc, tsn, rr, qkn, v, kt, qz, nmax, sums, rsum, pe_, pn, pt, oth, otl, x1, pX, pS) = W.tensors
    qkv_st, qkv_hi, qkv_lo = W.weights
    base, masks = K.base, K.masks
    S = W.sems
    g0 = layer * NW

    def steps(e, step):
        with e.Fori(0, NW // 4 - 1) as it:
            for j in range(4):
                step(it * 4 + j, j, it)
        for j in range(4):
            step(NW - 4 + j, j, NW // 4 - 1)

    def ahead(w, j, it, n):
        if isinstance(w, int) and w + n >= NW:
            return None
        return w + n, (j + n) % 4, it + (j + n) // 4

    with nc.Block() as block:
        @block.sync
        def _(sp):
            def load(w, j, it):
                r0 = stage_row(2 * layer, w)
                sp.dma_start(xt[:, j], X[bass.ds(r0, P), :]).then_inc(S["x_loaded"][j], 16)
                sp.dma_start(hs[:, j], X[bass.ds(r0 - 1, P), P:D]).then_inc(S["x_loaded"][j], 16)

            load(0, 0, 0)
            load(1, 1, 0)
            for z in range(3):
                cols = slice(z * INNER, (z + 1) * INNER)
                sp.dma_start(qkv_st[:, :, cols], wqkv[layer][:, cols].rearrange("(k p) n -> p k n", p=P))\
                  .then_inc(S["qkv_loaded"][z], 16)
            for w in range(2, 4):
                load(w, w, 0)

            def start_feed():
                HA = HC * P
                sp.wait_ge(S["w_split"], ONE + 4 * layer + 4)
                sp.wait_ge(F.sems["cleared"], ONE + 3 * layer + 1)
                for half, n in ((0, HA), (1, HID)):
                    sp.dma_start(qkv_st[:, :, half * HA:half * HA + n],
                                 w1[layer][:, half * HID:half * HID + n].rearrange("(k p) n -> p k n", p=P))\
                      .then_inc(F.sems["w1_loaded"], 16)
                for i in range(2):
                    sp.wait_ge(S["x1_stored"][i], ONE + (layer * (NW // 2) + SUP) * 16)
                for i in range(2):
                    load_h(sp, F, layer, X, i, i)

            def step(w, j, it):
                if isinstance(w, int) and w == NW - 4:
                    start_feed()
                sp.wait_ge(S["x1_ready"], ONE + 2 + g0 + w + 1)
                sp.dma_start(X[bass.ds(stage_row(2 * layer + 1, w), P), :], x1[:, j % 2])\
                  .then_inc(S["x1_stored"][j % 2], 16)
                nxt = ahead(w, j, it, 4)
                if nxt:
                    load(*nxt)

            steps(sp, step)
            for i in range(2):
                sp.wait_ge(S["x1_stored"][i], ONE + (layer + 1) * (NW // 2) * 16)
            sp.sem_inc(K.passed, 1)

        @block.gpsimd
        def _(pool):
            def rotated(w, j, it):
                pool.wait_ge(S["k_copied"], ONE + g0 + w + 1)
                pool.wait_ge(S["added"], ONE + g0 + w)
                t = w % TPB
                for z in range(2):
                    src = qk[:, j % 2, z * INNER:(z + 1) * INNER].rearrange("p (h f d) -> p h f d", f=2, d=LD // 2)
                    dst = tsn[:, z * INNER:(z + 1) * INNER].rearrange("p (h f d) -> p h f d", f=2, d=LD // 2)
                    s = tab[:, t, 2 * z + 1].rearrange("p (f d) -> p f d", f=2)[:, None].broadcast_to([P, LH, 2, LD // 2])
                    pool.tensor_tensor(dst, src[:, :, ::-1, :], s, ALU.mult).then_inc(S["ts_ready"], 1)

            def inverse_norm(w, j, it):
                pool.wait_ge(S["ss_ready"], ONE + g0 + w + 1)
                pool.sem_inc(K.passed, 1)
                pool.tensor_scalar(ssc[:, :], ss[:, j % 2], 1e-24, None, ALU.max).then_inc(S["ssc_ready"], 1)
                pool.wait_ge(S["ssc_ready"], ONE + g0 + w + 1)
                pool.tensor_tensor(rs[:, j % 2], ssc[:, :], K.mhalf[:, :], ALU.pow).then_inc(S["rs_ready"], 1)

            def add(w, j, it):
                pool.wait_ge(S["tc_ready"], ONE + g0 + w + 1)
                pool.wait_ge(S["ts_ready"], ONE + 2 * (g0 + w) + 2)
                pool.wait_ge(S["qkn_ready"], ONE + g0 + w)
                pool.tensor_tensor(rr[:, :], tc[:, :], tsn[:, :], ALU.add).then_inc(S["added"], 1)

            def rope(nxt):
                if nxt:
                    rotated(*nxt)
                    add(*nxt)
                    inverse_norm(*nxt)

            pool.memset(qz[:, :, :], 0.0).then_inc(S["cleared"], 1)
            pool.memset(kt[:, :, 1], 0.0).then_inc(S["cleared"], 1)
            pool.memset(v[:, 3], 0.0).then_inc(S["cleared"], 1)
            pool.wait_ge(S["w_loaded"], ONE + (layer + 1) * 2 * 16)
            def table(t0, t1):
                pool.tensor_tensor(tab[:, t0:t1].rearrange("p t f d -> p t (f d)"),
                                   base[:, t0:t1].rearrange("p t f d -> p t (f d)"),
                                   scales[:, :, :].rearrange("p f d -> p (f d)")[:, None, :]
                                   .broadcast_to([P, t1 - t0, 4 * LD]), ALU.mult).then_inc(S["tab_ready"], 1)

            table(0, 2)
            pool.wait_ge(S["tab_ready"], ONE + 2 * layer + 1)
            rope((0, 0, 0))
            rope((1, 1, 0))
            table(2, TPB)
            pool.wait_ge(S["tab_ready"], ONE + 2 * layer + 2)
            pool.sem_inc(K.passed, 1)
            pool.wait_ge(S["w_split"], ONE + 4 * layer + 4)
            pool.sem_inc(K.passed, 1)
            pool.memset(qkv_st[:, :, HC * P + HID:2 * HC * P], 0.0).then_inc(F.sems["cleared"], 1)

            def step(w, j, it):
                rope(ahead(w, j, it, 2))

            steps(pool, step)

        @block.scalar
        def _(act):

            act.dma_start(scales[:, :, :], qk_scales[layer][None].broadcast_to([P, 4, LD])).then_inc(S["w_loaded"], 16)
            act.dma_start(wo_st[:, :, :], wo[layer].rearrange("(k p) n -> p k n", p=P)).then_inc(S["w_loaded"], 16)

            def turned(w, j, it):
                act.wait_ge(S["t_ready"], ONE + g0 + w + 1)
                act.activation(thi[:, j % 2], pX[:, 0, 0:D].rearrange("p (k t) -> p k t", k=KD), ACT.Copy)\
                   .then_inc(S["t_hi"], 1)

            def copy_q(w, j, it):
                act.wait_ge(S["q_ready"], ONE + g0 + w + 1)
                act.activation(qk[:, j % 2, 0:INNER], pX[:, 1], ACT.Copy).then_inc(S["q_copied"], 1)

            def copy_k(w, j, it):
                act.wait_ge(S["k_ready"], ONE + g0 + w + 1)
                act.activation(qk[:, j % 2, INNER:2 * INNER], pX[:, 2], ACT.Copy).then_inc(S["k_copied"], 1)

            def exps(w, j, it, hf):
                act.wait_ge(S["max_ready"], ONE + 2 * (g0 + w) + hf + 1)
                for h in range(4 * hf, 4 * hf + 4):
                    ins = act.activation(pe_[:, h], pS[:, h // 2, h % 2], ACT.Exp, bias=nmax[:, h:h + 1],
                                         accum_out=sums[:, h:h + 1])
                ins.then_inc(S["exp_done"], 1)

            def copy_p(w, j, it, ch):
                act.wait_ge(S["pt_ready"], ONE + 4 * (g0 + w) + ch + 1)
                act.activation(pt[:, ch], pX[:, (0, 1, 3, 0)[ch]], ACT.Copy).then_inc(S["pt_even"], 1)

            def copy_out(w, j, it):
                act.wait_ge(S["ot_ready"], ONE + g0 + w + 1)
                act.activation(oth[:, :], pX[:, 2], ACT.Copy).then_inc(S["ot_hi"], 1)

            def copy_kt(w, j, it):
                act.wait_ge(S["kt_ready"], ONE + g0 + w + 1)
                act.activation(kt[:, :, j % 2], pX[:, 1].rearrange("p (c t) -> p c t", c=4), ACT.Copy)\
                   .then_inc(S["kt_copied"], 1)

            def squares(w, j, it):
                act.wait_ge(S["k_copied"], ONE + g0 + w + 1)
                act.wait_ge(S["ss_ready"], ONE + g0 + w)
                act.activation(sq[:, :], qk[:, j % 2], ACT.Square).then_inc(S["sq_ready"], 1)

            def copy_v(w, j, it):
                act.wait_ge(S["v_ready"], ONE + g0 + w + 1)
                act.activation(v[:, j], pX[:, 3], ACT.Copy).then_inc(S["v_copied"], 1)

            def copy_qz(w, j, it):
                act.wait_ge(S["qt_ready"], ONE + g0 + w + 1)
                for r in range(2):
                    rows = slice(r * LD, (r + 1) * LD)
                    ins = act.activation(qz[rows, r:LH:2, :], pX[rows, 3].rearrange("p (c t) -> p c t", c=4), ACT.Copy)
                ins.then_inc(S["qt_copied"], 1)

            act.wait_ge(S["cleared"], ONE + 3 * layer + 3)
            turned(0, 0, 0)
            for z in range(3):
                act.wait_ge(S["qkv_loaded"][z], ONE + (layer + 1) * 16)
                act.activation(qkv_hi[:, :, z * INNER:(z + 1) * INNER], qkv_st[:, :, z * INNER:(z + 1) * INNER],
                               ACT.Copy).then_inc(S["w_hi"], 1)
                if z == 0:
                    turned(1, 1, 0)
            for w in range(2):
                copy_q(w, w, 0)
                copy_k(w, w, 0)
                copy_v(w, w, 0)
                squares(w, w, 0)
                if w == 0:
                    act.wait_ge(S["w_loaded"], ONE + (layer + 1) * 2 * 16)
                    act.activation(wo_hi[:, :, :], wo_st[:, :, :], ACT.Copy).then_inc(S["w_hi"], 1)
            copy_kt(0, 0, 0)
            copy_qz(0, 0, 0)
            turned(2, 2, 0)

            def step(w, j, it):
                a1, a2, a3 = (ahead(w, j, it, n) for n in (1, 2, 3))
                exps(w, j, it, 0)
                if a2:
                    copy_q(*a2)
                exps(w, j, it, 1)
                if a2:
                    copy_k(*a2)
                copy_p(w, j, it, 0)
                if a2:
                    copy_v(*a2)
                copy_p(w, j, it, 2)
                if a2:
                    squares(*a2)
                if a1:
                    copy_kt(*a1)
                copy_out(w, j, it)
                if a1:
                    copy_qz(*a1)
                if a3:
                    turned(*a3)

            steps(act, step)

        @block.vector
        def _(dve):
            def split(i, lo, st, hi):
                dve.wait_ge(S["w_hi"], ONE + 4 * layer + i + 1)
                dve.tensor_tensor(lo, st, hi.bitcast(F32), ALU.subtract).then_inc(S["w_split"], 1)

            def lo_of(w, j, it):
                dve.wait_ge(S["t_hi"], ONE + g0 + w + 1)
                dve.tensor_tensor(tlo[:, j % 2], pX[:, 0, 0:D].rearrange("p (k t) -> p k t", k=KD),
                                  thi[:, j % 2].bitcast(F32), ALU.subtract).then_inc(S["t_lo"], 1)

            def cosines(w, j, it):
                dve.wait_ge(S["k_copied"], ONE + g0 + w + 1)
                dve.wait_ge(S["added"], ONE + g0 + w)
                t = w % TPB
                c = tab[:, t].rearrange("p (z f) d -> p z f d", z=2)[:, :, 0][:, :, None, :].broadcast_to([P, 2, LH, LD])
                dve.tensor_tensor(tc[:, :].rearrange("p (z h d) -> p z h d", z=2, h=LH),
                                  qk[:, j % 2].rearrange("p (z h d) -> p z h d", z=2, h=LH), c, ALU.mult)\
                   .then_inc(S["tc_ready"], 1)

            def sum_squares(w, j, it):
                dve.wait_ge(S["sq_ready"], ONE + g0 + w + 1)
                dve.wait_ge(S["ssc_ready"], ONE + g0 + w)
                dve.tensor_reduce(ss[:, j % 2], sq[:, :].rearrange("p (h d) -> p h d", d=LD), AX.X, ALU.add)\
                   .then_inc(S["ss_ready"], 1)

            def unit(w, j, it):
                dve.wait_ge(S["added"], ONE + g0 + w + 1)
                dve.wait_ge(S["rs_ready"], ONE + g0 + w + 1)
                dve.tensor_tensor(qkn[:, :].rearrange("p (h d) -> p h d", d=LD),
                                  rr[:, :].rearrange("p (h d) -> p h d", d=LD),
                                  rs[:, j % 2][:, :, None].broadcast_to([P, 2 * LH, LD]), ALU.mult)\
                   .then_inc(S["qkn_ready"], 1)

            def maxima(w, j, it, hf):
                dve.wait_ge(S["s_ready"], ONE + 2 * (g0 + w) + hf + 1)
                dve.tensor_reduce(nmax[:, 4 * hf:4 * hf + 4],
                                  pS[:, 2 * hf:2 * hf + 2].rearrange("p b h k -> p (b h) k"), AX.X, ALU.max,
                                  negate=True).then_inc(S["max_ready"], 1)

            def normalise(w, j, it, hf):
                dve.wait_ge(S["exp_done"], ONE + 2 + 2 * (g0 + w) + hf + 1)
                dve.reciprocal(rsum[:, 4 * hf:4 * hf + 4], sums[:, 4 * hf:4 * hf + 4]).then_inc(S["rsum_ready"], 1)
                dve.wait_ge(S["rsum_ready"], ONE + 2 * (g0 + w) + hf + 1)
                for h in range(4 * hf, 4 * hf + 4):
                    ins = dve.tensor_scalar(pn[:, h], pe_[:, h], rsum[:, h:h + 1], None, ALU.mult)
                ins.then_inc(S["pn_ready"], 1)

            def copy_p(w, j, it, ch):
                dve.wait_ge(S["pt_ready"], ONE + 4 * (g0 + w) + ch + 1)
                dve.tensor_copy(pt[:, ch], pX[:, (0, 1, 3, 0)[ch]]).then_inc(S["pt_odd"], 1)

            def lo_out(w, j, it):
                dve.wait_ge(S["ot_hi"], ONE + g0 + w + 1)
                dve.tensor_tensor(otl[:, :], pX[:, 2], oth[:, :].bitcast(F32), ALU.subtract).then_inc(S["ot_lo"], 1)

            def residual(w, j, it):
                dve.wait_ge(S["wo_ready"], ONE + g0 + w + 1)
                dve.wait_ge(S["x1_stored"][j % 2], ONE + (layer * (NW // 2) + (w // 2)) * 16)
                dve.tensor_tensor(x1[:, j % 2], pX[:, 0, 0:D], xt[:, j], ALU.add).then_inc(S["x1_ready"], 1)

            lo_of(0, 0, 0)
            for z in range(3):
                cols = slice(z * INNER, (z + 1) * INNER)
                split(z, qkv_lo[:, :, cols], qkv_st[:, :, cols], qkv_hi[:, :, cols])
                if z == 0:
                    lo_of(1, 1, 0)
            dve.wait_ge(S["tab_ready"], ONE + 2 * layer + 1)
            for w in range(2):
                cosines(w, w, 0)
                sum_squares(w, w, 0)
                if w == 0:
                    split(3, wo_lo[:, :, :], wo_st[:, :, :], wo_hi[:, :, :])
                if w == 0:
                    unit(0, 0, 0)
            maxima(0, 0, 0, 0)
            lo_of(2, 2, 0)
            dve.wait_ge(S["tab_ready"], ONE + 2 * layer + 2)
            maxima(0, 0, 0, 1)

            def step(w, j, it):
                a1, a2, a3 = (ahead(w, j, it, n) for n in (1, 2, 3))
                normalise(w, j, it, 0)
                if a1:
                    unit(*a1)
                normalise(w, j, it, 1)
                copy_p(w, j, it, 1)
                copy_p(w, j, it, 3)
                lo_out(w, j, it)
                if a2:
                    cosines(*a2)
                residual(w, j, it)
                if a2:
                    sum_squares(*a2)
                if a1:
                    maxima(*a1, 0)
                if a3:
                    lo_of(*a3)
                if a1:
                    maxima(*a1, 1)

            steps(dve, step)

        @block.tensor
        def _(pe):
            def turn_h(w, j, it):
                pe.wait_ge(S["x_loaded"][j], ONE + (layer * (NW // 4) + it + 1) * 32)
                pe.wait_ge(S["x1_ready"], ONE + g0 + w)
                pe.wait_ge(S["t_lo"], ONE + g0 + w)
                pe.transpose(pX[:, 0, 0:P], xt[:, j, 0:P], K.ident[:, :])
                pe.transpose(pX[:, 0, P:D], hs[:, j], K.ident[:, :]).then_inc(S["t_ready"], 1)

            def project(w, j, it):
                pe.wait_ge(S["t_lo"], ONE + g0 + w + 1)
                for z in range(3):
                    if z == 0:
                        pe.wait_ge(S["kt_copied"], ONE + g0 + w)
                        pe.wait_ge(S["q_copied"], ONE + g0 + w)
                    elif z == 1:
                        pe.wait_ge(S["ot_lo"], ONE + g0 + w)
                        pe.wait_ge(S["k_copied"], ONE + g0 + w)
                    else:
                        pe.wait_ge(S["qt_copied"], ONE + g0 + w)
                        pe.wait_ge(S["v_copied"], ONE + g0 + w)
                    cols = slice(z * INNER, (z + 1) * INNER)
                    if isinstance(w, int) and w == 0:
                        pe.wait_ge(S["w_split"], ONE + 4 * layer + z + 1)
                    terms = [(t, m, k) for k in range(KD) for t, m in ((thi, qkv_hi), (thi, qkv_lo), (tlo, qkv_hi))]
                    for i, (t, m, k) in enumerate(terms):
                        ins = pe.matmul(pX[:, 1 + z], t[:, j % 2, k], m[:, k, cols], start=i == 0,
                                        stop=i == len(terms) - 1)
                    ins.then_inc((S["q_ready"], S["k_ready"], S["v_ready"])[z], 1)

            def turn_p(w, j, it, ch, bank):
                pe.wait_ge(S["pn_ready"], ONE + 2 * (g0 + w) + ch // 2 + 1)
                for hh in range(2):
                    for s in range(2):
                        o = (2 * hh + s) * P
                        ins = pe.transpose(pX[:, bank, o:o + P], pn[:, 2 * ch + hh, s * P:(s + 1) * P], K.ident[:, :])
                ins.then_inc(S["pt_ready"], 1)

            def values(w, j, it, ch):
                if ch % 2 == 0:
                    pe.wait_ge(S["pt_even"], ONE + 2 * (g0 + w) + ch // 2 + 1)
                else:
                    pe.wait_ge(S["pt_odd"], ONE + 2 * (g0 + w) + ch // 2 + 1)
                for s in range(2):
                    vj = j if s == j % 2 else (j - 1) % 4
                    for hh in range(2):
                        h, o = 2 * ch + hh, (2 * hh + s) * P
                        ins = pe.matmul(pX[hh * LD:(hh + 1) * LD, 2, ch * P:(ch + 1) * P], v[:, vj, h * LD:(h + 1) * LD],
                                        pt[:, ch, o:o + P], start=s == 0, stop=s == 1)
                if ch == 3:
                    ins.then_inc(S["ot_ready"], 1)

            def attend(w, j, it):
                last = min(w + 3, NW) if isinstance(w, int) else w + 3
                pe.wait_ge(S["x1_ready"], ONE + 2 + g0 + w)
                turn_p(w, j, it, 0, 0)
                pe.wait_ge(S["q_copied"], ONE + g0 + last)
                pe.wait_ge(S["kt_copied"], ONE + 1 + g0 + w + 1)
                turn_p(w, j, it, 1, 1)
                pe.wait_ge(S["k_copied"], ONE + g0 + last)
                pe.wait_ge(S["ot_lo"], ONE + 2 + g0 + w)
                values(w, j, it, 0)
                pe.wait_ge(S["v_copied"], ONE + g0 + last)
                pe.wait_ge(S["qt_copied"], ONE + 1 + g0 + w + 1)
                turn_p(w, j, it, 2, 3)
                values(w, j, it, 1)
                turn_p(w, j, it, 3, 0)
                values(w, j, it, 2)
                nxt = ahead(w, j, it, 1)
                if nxt:
                    turn_k(*nxt)
                    turn_q(*nxt)
                values(w, j, it, 3)

            def turn_k(w, j, it):
                last = min(w + 2, NW) if isinstance(w, int) else w + 2
                pe.wait_ge(S["qkn_ready"], ONE + g0 + w + 1)
                pe.wait_ge(S["q_copied"], ONE + g0 + last)
                for ch in range(4):
                    ins = pe.transpose(pX[:, 1, ch * P:(ch + 1) * P], qkn[:, INNER + ch * P:INNER + (ch + 1) * P],
                                       K.ident[:, :])
                ins.then_inc(S["kt_ready"], 1)

            def turn_q(w, j, it):
                last = min(w + 2, NW) if isinstance(w, int) else w + 2
                pe.wait_ge(S["v_copied"], ONE + g0 + last)
                for ch in range(4):
                    ins = pe.transpose(pX[:, 3, ch * P:(ch + 1) * P], qkn[:, ch * P:(ch + 1) * P], K.ident[:, :])
                ins.then_inc(S["qt_ready"], 1)

            def output(w, j, it):
                pe.wait_ge(S["ot_hi"], ONE + g0 + w + 1)
                terms = [(oth, m, k) for k in range(KI) for m in (wo_hi, wo_lo)] + [(otl, wo_hi, k) for k in range(KI)]
                for i, (t, m, k) in enumerate(terms):
                    if i == 2 * KI:
                        pe.wait_ge(S["ot_lo"], ONE + 2 + g0 + w + 1)
                    ins = pe.matmul(pX[:, 0, 0:D], t[:, k * P:(k + 1) * P], m[:, k], start=i == 0,
                                    stop=i == len(terms) - 1)
                ins.then_inc(S["wo_ready"], 1)

            def mask(w, j, it):
                kind = it % 2 if j == 0 else (2 if j % 2 else 1)
                for b in range(4):
                    pe.wait_ge(S["exp_done"], ONE + 2 * (g0 + w) + b // 2 + 1)
                    pe.matmul(pS[:, b].rearrange("p h k -> p (h k)"), K.identb[:, :], masks[:, kind], start=True,
                              stop=False)

            def score(w, j, it, hf):
                if hf == 0:
                    pe.wait_ge(S["kt_copied"], ONE + 1 + g0 + w + 1)
                    pe.wait_ge(S["qt_copied"], ONE + 1 + g0 + w + 1)
                for b in (2 * hf, 2 * hf + 1):
                    for hh in range(2):
                        ins = pe.matmul(pS[:, b, hh], qz[:, 2 * b + hh, :], kt[:, b].rearrange("p s t -> p (s t)"),
                                        start=False, stop=hh == 1)
                ins.then_inc(S["s_ready"], 1)

            for w in range(2):
                turn_h(w, w, 0)
            for w in range(2):
                project(w, w, 0)
            pe.wait_ge(S["cleared"], ONE + 3 * layer + 3)
            pe.wait_ge(S["w_split"], ONE + 4 * layer + 4)
            turn_k(0, 0, 0)
            turn_q(0, 0, 0)
            mask(0, 0, 0)
            score(0, 0, 0, 0)
            turn_h(2, 2, 0)
            score(0, 0, 0, 1)

            def step(w, j, it):
                a1, a2, a3 = (ahead(w, j, it, n) for n in (1, 2, 3))
                if a2:
                    project(*a2)
                attend(w, j, it)
                if a1:
                    mask(*a1)
                output(w, j, it)
                if a1:
                    score(*a1, 0)
                if a3:
                    turn_h(*a3)
                if a1:
                    score(*a1, 1)

            steps(pe, step)


def phase_feed(nc, K, W, F, layer, X, ln_g, ln_b, b1, w2, b2):
    NS = SUPERS
    N = SUP * P
    HA = HC * P
    TAIL = HID - (HC - 1) * P
    (w2_st, w2_hi, w2_lo, b1a, b1g, lng, lnb, b2t, hh, xr, stt, mv, ve, rstd, hn, hf, thi, tlo, gl, af,
     ahi, alo, xb, x2, pT, pH, pO) = F.tensors
    w1_st, w1_hi, w1_lo = W.weights
    S = F.sems
    g0 = layer * NS

    def steps(e, step):
        with e.Fori(0, NS // 2 - 2) as it:
            step(it * 2 + 1, 1, it)
            step(it * 2 + 2, 0, it + 1)
        step(NS - 3, 1, NS // 2 - 2)
        step(NS - 2, 0, NS // 2 - 1)
        step(NS - 1, 1, NS // 2 - 1)
        step(NS, 0, NS // 2)

    def within(s, n):
        return None if isinstance(s, int) and s + n >= NS else s + n

    def chunks_of(w, part):
        half = slice(part * HA // 2, (part + 1) * HA // 2)
        return w[:, :, :].rearrange("p k (z c) -> p k z c", z=2)[:, :, :, half]

    with nc.Block() as block:
        @block.sync
        def _(sp):
            def load(dst, src, columns=False, sem="w_loaded"):
                sp.dma_start(dst, src, allow_slow_non_contiguous=columns).then_inc(S[sem], 16)

            def row(stage, s):
                return stage * ST_ROWS + s * N + s * SUP // TPB + 1

            load(lng[:, :], ln_g[layer].rearrange("(k p) -> p k", p=P), True, sem="ln_loaded")
            load(lnb[:, :], ln_b[layer].rearrange("(k p) -> p k", p=P), True, sem="ln_loaded")
            load(b2t[:, :], b2[layer][None, :].broadcast_to([P, D]))
            load(b1a[:, :], b1[layer][0:HA].rearrange("(c p) -> p c", p=P), True)
            sp.wait_ge(S["cleared"], ONE + 3 * layer + 3)
            load(w2_st[:, 0:HC - 1], w2[layer][0:(HC - 1) * P].rearrange("(c p) n -> p c n", p=P))
            load(w2_st[0:TAIL, HC - 1], w2[layer][(HC - 1) * P:HID])
            load(b1g[:, 0:HC - 1], b1[layer][HID:HID + (HC - 1) * P].rearrange("(c p) -> p c", p=P), True)
            load(b1g[0:TAIL, HC - 1:HC], b1[layer][HID + (HC - 1) * P:2 * HID].rearrange("(p c) -> p c", c=1), True)

            def load_x(s, j):
                sp.dma_start(xr[:, j], X[bass.ds(row(2 * layer + 1, s), N), :].rearrange("(n p) d -> p n d", p=P))\
                  .then_inc(S["x_loaded"][j], 16)

            def store(s, j):
                sp.wait_ge(S["x2_ready"], ONE + 2 + SUP * (g0 + s + 1))
                sp.dma_start(X[bass.ds(row(2 * layer + 2, s), N), :].rearrange("(n p) d -> p n d", p=P), x2[:, j])\
                  .then_inc(S["x2_stored"][j], 16)

            load_x(0, 0)
            load_x(1, 1)
            sp.wait_ge(S["hn_ready"], ONE + g0 + 1)
            load_h(sp, F, layer, X, 2, 0)

            def step(s, j, it):
                if within(s, 2) is not None:
                    sp.wait_ge(S["hn_ready"], ONE + g0 + s + 1)
                    load_h(sp, F, layer, X, s + 2, j)
                store(s - 1, 1 - j)
                if within(s, 1) is not None:
                    sp.wait_ge(S["xb_ready"], ONE + g0 + s)
                    load_x(s + 1, 1 - j)

            steps(sp, step)
            for j in range(2):
                sp.wait_ge(S["x2_stored"][j], ONE + (layer + 1) * (NS // 2) * 16)
            sp.sem_inc(K.passed, 1)

        @block.gpsimd
        def _(pool):
            pool.memset(w2_st[:, HC - 1], 0.0).then_inc(S["cleared"], 1)
            pool.memset(b1g[:, :], 0.0).then_inc(S["cleared"], 1)

            def rstd_of(s, j):
                pool.wait_ge(S["mv_ready"], ONE + (g0 + s + 1) * SUP)
                pool.sem_inc(K.passed, 1)
                pool.tensor_scalar(ve[:, j], mv[:, j, :, 1], 1e-5, None, ALU.add).then_inc(S["ve_ready"], 1)
                pool.wait_ge(S["ve_ready"], ONE + g0 + s + 1)
                pool.tensor_tensor(rstd[:, j], ve[:, j], K.mhalf[:, 0:SUP], ALU.pow).then_inc(S["rstd_ready"], 1)

            def add_b2(s, j, it):
                pool.wait_ge(S["x_loaded"][j], ONE + (layer * (NS // 2) + it + 1) * 16)
                pool.wait_ge(S["x2_ready"], ONE + 2 + SUP * (g0 + s))
                pool.tensor_tensor(xb[:, j], xr[:, j], b2t[:, None, :].broadcast_to([P, SUP, D]), ALU.add)\
                    .then_inc(S["xb_ready"], 1)

            def split(s, j, ch):
                u = (g0 + s) * HC + ch
                pool.wait_ge(S["act_ready"], ONE + 2 + u + 1)
                pool.sem_inc(K.passed, 1)
                pool.tensor_scalar(ahi[:, j, ch], af[:, ch % 2], 1.0, None, ALU.mult).then_inc(S["a_hi"], 1)
                pool.wait_ge(S["a_hi"], ONE + u + 1)
                pool.tensor_tensor(alo[:, j, ch], af[:, ch % 2], ahi[:, j, ch].bitcast(F32), ALU.subtract)\
                    .then_inc(S["a_lo"], 1)

            rstd_of(0, 0)
            rstd_of(1, 1)

            def body(s, j, it):
                for ch in range(HC):
                    split(s, j, ch)
                    if ch == 1 and within(s, 2) is not None:
                        rstd_of(s + 2, j)

            body(0, 0, 0)

            def step(s, j, it):
                if within(s, 0) is not None:
                    body(s, j, it)

            def whole(s, j, it):
                add_b2(s - 1, 1 - j, it - 1 + j)
                step(s, j, it)

            steps(pool, whole)

        @block.scalar
        def _(act):
            act.wait_ge(S["w1_loaded"], ONE + (layer + 1) * 2 * 16)
            act.wait_ge(S["cleared"], ONE + 3 * layer + 3)
            for part in range(2):
                act.activation(chunks_of(w1_hi, part), chunks_of(w1_st, part), ACT.Copy).then_inc(S["w_hi"], 1)

            def turned(s, j):
                act.wait_ge(S["t_ready"], ONE + g0 + s + 1)
                act.wait_ge(S["t_lo"], ONE + g0 + s)
                for k in range(KD):
                    ins = act.activation(hf[:, k], pT[:, k], ACT.Identity, bias=lnb[:, k:k + 1], scale=lng[:, k:k + 1])
                    ins.then_inc(S["hf_ready"], 1)
                act.wait_ge(S["hf_ready"], ONE + KD * (g0 + s + 1))
                act.activation(thi[:, j], hf[:, :, :], ACT.Copy).then_inc(S["t_hi"], 1)

            def gelus(s, j, midway=lambda: None):
                for ch in range(HC):
                    if ch == HC // 2:
                        midway()
                    u = (g0 + s) * HC + ch
                    act.wait_ge(S["g_ready"], ONE + u + 1)
                    act.wait_ge(S["act_ready"], ONE + u + 1)
                    act.activation(gl[:, ch % 2], pH[:, ch % 2, 1], ACT.Gelu, bias=b1g[:, ch:ch + 1])\
                       .then_inc(S["gelu_done"], 1)

            act.wait_ge(S["ln_loaded"], ONE + (layer + 1) * 2 * 16)
            turned(0, 0)
            act.wait_ge(S["w_loaded"], ONE + (layer + 1) * 6 * 16)
            act.activation(w2_hi[:, :, :], w2_st[:, :, :], ACT.Copy).then_inc(S["w_hi"], 1)
            gelus(0, 0, lambda: turned(1, 1))

            def step(s, j, it):
                if within(s, 1) is not None:
                    turned(s + 1, 1 - j)
                if within(s, 0) is not None:
                    gelus(s, j)

            steps(act, step)

        @block.vector
        def _(dve):
            def moments(s, j, it):
                dve.wait_ge(S["h_loaded"][j], ONE + (layer * (NS // 2) + it + 1) * 32)
                for n in range(SUP):
                    dve.bn_stats(stt[:, j, n], hh[:, j, n]).then_inc(S["stats"], 1)
                dve.wait_ge(S["stats"], ONE + (g0 + s) * SUP + SUP)
                dve.sem_inc(K.passed, 1)
                for n in range(SUP):
                    dve.bn_aggr(mv[:, j, n], stt[:, j, n]).then_inc(S["mv_ready"], 1)

            def normalise(s, j, it):
                dve.wait_ge(S["rstd_ready"], ONE + g0 + s + 1)
                for n in range(SUP):
                    ins = dve.tensor_scalar(hn[:, j, n], hh[:, j, n], mv[:, j, n, 0:1], rstd[:, j, n:n + 1],
                                            ALU.subtract, ALU.mult)
                ins.then_inc(S["hn_ready"], 1)

            def lo_of(s, j):
                dve.wait_ge(S["t_hi"], ONE + g0 + s + 1)
                dve.tensor_tensor(tlo[:, j], hf[:, :, :], thi[:, j].bitcast(F32), ALU.subtract).then_inc(S["t_lo"], 1)

            def gated(s, j, ch):
                u = (g0 + s) * HC + ch
                dve.wait_ge(S["gelu_done"], ONE + u + 1)
                dve.wait_ge(S["a_lo"], ONE + u)
                dve.scalar_tensor_tensor(af[:, ch % 2], pH[:, ch % 2, 0], b1a[:, ch:ch + 1], gl[:, ch % 2],
                                         ALU.add, ALU.mult).then_inc(S["act_ready"], 1)

            def residual(s, j, it):
                dve.wait_ge(S["xb_ready"], ONE + g0 + s + 1)
                dve.wait_ge(S["x2_stored"][j], ONE + (layer * (NS // 2) + it) * 16)
                for n in range(SUP):
                    dve.wait_ge(S["o_ready"], ONE + (g0 + s) * SUP + n + 1)
                    dve.tensor_tensor(x2[:, j, n], pO[:, n % 2, 0:D], xb[:, j, n], ALU.add).then_inc(S["x2_ready"], 1)

            def body(s, j, it):
                for ch in range(HC):
                    gated(s, j, ch)
                    if within(s, 2) is not None:
                        if ch == 2:
                            moments(s + 2, j, it + 1)
                        elif ch == 3:
                            normalise(s + 2, j, it + 1)

            moments(0, 0, 0)
            normalise(0, 0, 0)
            for part in range(2):
                dve.wait_ge(S["w_hi"], ONE + 3 * layer + part + 1)
                dve.tensor_tensor(chunks_of(w1_lo, part), chunks_of(w1_st, part), chunks_of(w1_hi, part).bitcast(F32),
                                  ALU.subtract).then_inc(S["w_split"], 1)
                if part == 0:
                    lo_of(0, 0)
            moments(1, 1, 0)
            gated(0, 0, 0)
            normalise(1, 1, 0)
            gated(0, 0, 1)
            dve.wait_ge(S["w_hi"], ONE + 3 * layer + 3)
            dve.tensor_tensor(w2_lo[:, :, :], w2_st[:, :, :], w2_hi[:, :, :].bitcast(F32), ALU.subtract)\
               .then_inc(S["w_split"], 1)
            for ch in range(2, HC):
                gated(0, 0, ch)
                if ch == 2:
                    moments(2, 0, 1)
                elif ch == HC // 2:
                    lo_of(1, 1)
                    normalise(2, 0, 1)

            def step(s, j, it):
                if within(s, 1) is not None:
                    lo_of(s + 1, 1 - j)
                if within(s, 0) is not None:
                    body(s, j, it)
                residual(s - 1, 1 - j, it - 1 + j)

            steps(dve, step)

        @block.tensor
        def _(pe):
            def turn(s, j):
                pe.wait_ge(S["hn_ready"], ONE + g0 + s + 1)
                pe.wait_ge(S["hf_ready"], ONE + KD * (g0 + s))
                for k in range(KD):
                    for n in range(SUP):
                        ins = pe.transpose(pT[:, k, n * P:(n + 1) * P], hn[:, j, n, k * P:(k + 1) * P], K.ident[:, :])
                ins.then_inc(S["t_ready"], 1)

            def up(s, j, midway=lambda: None):
                pe.wait_ge(S["t_lo"], ONE + g0 + s + 1)
                for ch in range(HC):
                    if ch == HC // 2:
                        midway()
                    u = (g0 + s) * HC + ch
                    pe.wait_ge(S["act_ready"], ONE + u + 1)
                    for half in range(2):
                        cols = slice(half * HA + ch * P, half * HA + (ch + 1) * P)
                        terms = [(m, t, k) for k in range(KD) for m, t in ((w1_hi, thi), (w1_hi, tlo), (w1_lo, thi))]
                        for i, (m, t, k) in enumerate(terms):
                            ins = pe.matmul(pH[:, ch % 2, half], m[:, k, cols], t[:, j, k], start=i == 0,
                                            stop=i == len(terms) - 1)
                    ins.then_inc(S["g_ready"], 1)

            def down(s, j):
                for n in range(SUP):
                    pe.wait_ge(S["a_lo"], ONE + 1 + (g0 + s) * HC + HC)
                    pe.wait_ge(S["x2_ready"], ONE + (g0 + s) * SUP + n + 1)
                    ts = slice(n * P, (n + 1) * P)
                    terms = [(t, m, ch) for ch in range(HC) for t, m in ((ahi, w2_hi), (ahi, w2_lo), (alo, w2_hi))]
                    for i, (t, m, ch) in enumerate(terms):
                        ins = pe.matmul(pO[:, n % 2, 0:D], t[:, j, ch, ts], m[:, ch], start=i == 0,
                                        stop=i == len(terms) - 1)
                    ins.then_inc(S["o_ready"], 1)

            turn(0, 0)
            pe.wait_ge(S["w_split"], ONE + 3 * layer + 1)

            def midway():
                pe.wait_ge(S["w_split"], ONE + 3 * layer + 2)
                turn(1, 1)

            up(0, 0, midway)
            pe.wait_ge(S["w_split"], ONE + 3 * layer + 3)
            pe.sem_inc(K.passed, 1)

            def step(s, j, it):
                if within(s, 1) is not None:
                    turn(s + 1, 1 - j)
                if within(s, 0) is not None:
                    up(s, j)
                down(s - 1, 1 - j)

            steps(pe, step)


def phase_output(nc, K, AO, X, x, wo, out):
    with ExitStack() as c:
        sb = lambda n, s, d: c.enter_context(nc.sbuf_tensor(n, s, d))
        ps = lambda n, s, d: c.enter_context(nc.psum_tensor(n, s, d))
        mine = []

        def sem(name):
            mine.append(c.enter_context(nc.semaphore(name)))
            return mine[-1]

        wst = sb("p3_wst", [P, KD, D], F32)
        whi = sb("p3_whi", [P, KD, D], F32R)
        wlo = sb("p3_wlo", [P, KD, D], F32R)
        a = sb("p3_a", [P, 2, SUP, D], F32)
        f = sb("p3_f", [P, 2, SUP, D], F32)
        xi = sb("p3_x", [P, 2, SUP, D], F32)
        thi = sb("p3_thi", [P, 2, KD, SUP * P], F32R)
        tlo = sb("p3_tlo", [P, 2, KD, SUP * P], F32R)
        gate = sb("p3_gate", [P, 2, SUP, D], F32)
        prod = sb("p3_prod", [P, 2, SUP, D], F32)
        res = sb("p3_res", [P, 2, SUP, D], F32)
        pT = ps("p3_pT", [P, KD, 512], F32)
        pO = ps("p3_pO", [P, 2, 2, D], F32)
        w_loaded, w_hi, w_split = sem("p3_w_loaded"), sem("p3_w_hi"), sem("p3_w_split")
        a_loaded = [sem(f"p3_a_loaded{i}") for i in range(2)]
        f_loaded = [sem(f"p3_f_loaded{i}") for i in range(2)]
        x_loaded = [sem(f"p3_x_loaded{i}") for i in range(2)]
        stored = [sem(f"p3_stored{i}") for i in range(2)]
        t_ready, t_hi, t_lo = sem("p3_t_ready"), sem("p3_t_hi"), sem("p3_t_lo")
        o_ready, prod_ready, gate_ready, res_ready = (
            sem("p3_o_ready"), sem("p3_prod_ready"), sem("p3_gate_ready"), sem("p3_res_ready"))
        tiles = lambda d: d.rearrange("(s n p) d -> s p n d", n=SUP, p=P)
        block = c.enter_context(nc.Block())

        def steps(e, step):
            with e.Fori(0, SUPERS // 2 - 1) as it:
                for j in range(2):
                    step(it * 2 + j, j, it, True)
            step(SUPERS - 2, 0, SUPERS // 2 - 1, True)
            step(SUPERS - 1, 1, SUPERS // 2 - 1, False)

        @block.sync
        def _(sp):
            def load_a(s, j):
                sp.dma_start(a[:, j], tiles(AO)[s]).then_inc(a_loaded[j], 16)

            def load_f(s, j):
                r0 = 2 * LAYERS * ST_ROWS + s * SUP * P + s // 2 + 1
                sp.dma_start(f[:, j], X[bass.ds(r0, SUP * P), :].rearrange("(n p) d -> p n d", p=P))\
                  .then_inc(f_loaded[j], 16)

            def load_x(s, j):
                sp.dma_start(xi[:, j], tiles(x)[s]).then_inc(x_loaded[j], 16)

            load_a(0, 0)
            sp.dma_start(wst[:, :, :], wo.rearrange("(k p) n -> p k n", p=P)).then_inc(w_loaded, 16)
            load_a(1, 1)
            for s in range(2):
                load_f(s, s)
                load_x(s, s)

            def step(s, j, it, more):
                ahead = not (isinstance(s, int) and s + 2 >= SUPERS)
                if ahead:
                    sp.wait_ge(t_ready, ONE + s + 1)
                    load_a(s + 2, j)
                    sp.wait_ge(gate_ready, ONE + s + 1)
                    load_f(s + 2, j)
                sp.wait_ge(res_ready, ONE + s + 1)
                sp.dma_start(tiles(out)[s], res[:, j]).then_inc(stored[j], 16)
                if ahead:
                    load_x(s + 2, j)

            steps(sp, step)
            for j in range(2):
                sp.wait_ge(stored[j], ONE + 16 * SUPERS // 2)

        @block.scalar
        def _(act):
            act.wait_ge(w_loaded, ONE + 16)
            act.activation(whi[:, :, :], wst[:, :, :], ACT.Copy).then_inc(w_hi, 1)

            def hi_of(s, j):
                act.wait_ge(t_ready, ONE + s + 1)
                act.activation(thi[:, j], pT[:, :, :], ACT.Copy).then_inc(t_hi, 1)

            hi_of(0, 0)

            def step(s, j, it, more):
                if more:
                    hi_of(s + 1, 1 - j)
                act.wait_ge(f_loaded[j], ONE + (it + 1) * 16)
                act.wait_ge(prod_ready, ONE + 2 * s)
                act.activation(gate[:, j], f[:, j], ACT.Silu).then_inc(gate_ready, 1)

            steps(act, step)

        @block.vector
        def _(dve):
            start_at_one(dve, mine)
            dve.wait_ge(w_hi, ONE + 1)
            dve.tensor_tensor(wlo[:, :, :], wst[:, :, :], whi[:, :, :].bitcast(F32), ALU.subtract).then_inc(w_split, 1)

            def lo_of(s, j):
                dve.wait_ge(t_hi, ONE + s + 1)
                dve.tensor_tensor(tlo[:, j], pT[:, :, :], thi[:, j].bitcast(F32), ALU.subtract).then_inc(t_lo, 1)

            lo_of(0, 0)
            dve.sem_inc(prod_ready, 2)

            def step(s, j, it, more):
                if more:
                    lo_of(s + 1, 1 - j)
                dve.wait_ge(gate_ready, ONE + s + 1)
                for v in range(2):
                    dve.wait_ge(o_ready, ONE + 2 * s + v + 1)
                    dve.tensor_tensor(prod[:, j, 2 * v:2 * v + 2], pO[:, v], gate[:, j, 2 * v:2 * v + 2],
                                      ALU.mult).then_inc(prod_ready, 1)
                dve.wait_ge(prod_ready, ONE + 2 + 2 * s + 2)
                dve.wait_ge(stored[j], ONE + it * 16)
                dve.wait_ge(x_loaded[j], ONE + (it + 1) * 16)
                dve.tensor_tensor(res[:, j], prod[:, j], xi[:, j], ALU.add).then_inc(res_ready, 1)

            steps(dve, step)

        @block.tensor
        def _(pe):
            def turn(s, j, it):
                pe.wait_ge(a_loaded[j], ONE + (it + 1) * 16)
                pe.wait_ge(t_lo, ONE + s)
                for k in range(KD):
                    for n in range(SUP):
                        ins = pe.transpose(pT[:, k, n * P:(n + 1) * P], a[:, j, n, k * P:(k + 1) * P], K.ident[:, :])
                ins.then_inc(t_ready, 1)

            turn(0, 0, 0)
            pe.wait_ge(w_split, ONE + 1)

            def step(s, j, it, more):
                pe.wait_ge(t_lo, ONE + s + 1)
                for n in range(SUP):
                    v, o = n // 2, n % 2
                    if n == 1 and more:
                        turn(s + 1, 1 - j, it + j)
                    if o == 0:
                        pe.wait_ge(prod_ready, ONE + 2 * s + v + 1)
                    ts = slice(n * P, (n + 1) * P)
                    terms = [(t, w, k) for k in range(KD) for t, w in ((thi, whi), (thi, wlo), (tlo, whi))]
                    for i, (t, w, k) in enumerate(terms):
                        ins = pe.matmul(pO[:, v, o], t[:, j, k, ts], w[:, k], start=i == 0, stop=i == len(terms) - 1)
                    if o == 1:
                        ins.then_inc(o_ready, 1)

            steps(pe, step)


def semaphores(c, nc, prefix, names, rings):
    sems = {n: c.enter_context(nc.semaphore(prefix + n)) for n in names}
    sems.update({n: [c.enter_context(nc.semaphore(f"{prefix}{n}{i}")) for i in range(k)] for n, k in rings.items()})
    return sems


def start_at_one(e, sems):
    for s in sems:
        for x in (s if isinstance(s, list) else [s]):
            e.sem_inc(x, ONE)


class Named:
    pass


def window_tensors(nc, c, W):
    sb = lambda n, s, d: c.enter_context(nc.sbuf_tensor("w_" + n, s, d))
    ps = lambda n, s, d: c.enter_context(nc.psum_tensor("w_" + n, s, d))
    W.tensors = (
        sb("wo_st", [P, KI, D], F32), sb("wo_hi", [P, KI, D], F32R), sb("wo_lo", [P, KI, D], F32R),
        sb("scales", [P, 4, LD], F32), sb("tab", [P, TPB, 4, LD], F32),
        sb("xt", [P, 4, D], F32), sb("hs", [P, 4, P], F32),
        sb("thi", [P, 2, KD, P], F32R), sb("tlo", [P, 2, KD, P], F32R),
        sb("qk", [P, 2, 2 * INNER], F32), sb("sq", [P, 2 * INNER], F32),
        sb("ss", [P, 2, 2 * LH], F32), sb("ssc", [P, 2 * LH], F32), sb("rs", [P, 2, 2 * LH], F32),
        sb("tc", [P, 2 * INNER], F32), sb("tsn", [P, 2 * INNER], F32), sb("rr", [P, 2 * INNER], F32),
        sb("qkn", [P, 2 * INNER], F32),
        sb("v", [P, 4, INNER], F32), sb("kt", [P, KI, 2, P], F32), sb("qz", [P, LH, P], F32),
        sb("nmax", [P, LH], F32), sb("sums", [P, LH], F32), sb("rsum", [P, LH], F32),
        sb("pe", [P, LH, 2 * P], F32), sb("pn", [P, LH, 2 * P], F32), sb("pt", [P, 4, 512], F32),
        sb("oth", [P, INNER], F32R), sb("otl", [P, INNER], F32R), sb("x1", [P, 2, D], F32),
        ps("pX", [P, 4, 512], F32), ps("pS", [P, 4, 2, 2 * P], F32))


def feed_tensors(nc, c, F):
    sb = lambda n, s, d: c.enter_context(nc.sbuf_tensor("f_" + n, s, d))
    ps = lambda n, s, d: c.enter_context(nc.psum_tensor("f_" + n, s, d))
    N = SUP * P
    F.tensors = (
        sb("w2_st", [P, HC, D], F32), sb("w2_hi", [P, HC, D], F32R), sb("w2_lo", [P, HC, D], F32R),
        sb("b1a", [P, HC], F32), sb("b1g", [P, HC], F32), sb("lng", [P, KD], F32), sb("lnb", [P, KD], F32),
        sb("b2t", [P, D], F32), F.hh, sb("xr", [P, 2, SUP, D], F32),
        sb("stt", [P, 2, SUP, 6], F32), sb("mv", [P, 2, SUP, 2], F32), sb("ve", [P, 2, SUP], F32),
        sb("rstd", [P, 2, SUP], F32), sb("hn", [P, 2, SUP, D], F32), sb("hf", [P, KD, N], F32),
        sb("thi", [P, 2, KD, N], F32R), sb("tlo", [P, 2, KD, N], F32R), sb("gl", [P, 2, N], F32),
        sb("af", [P, 2, N], F32), sb("ahi", [P, 2, HC, N], F32R), sb("alo", [P, 2, HC, N], F32R),
        sb("xb", [P, 2, SUP, D], F32), sb("x2", [P, 2, SUP, D], F32),
        ps("pT", [P, KD, N], F32), ps("pH", [P, 2, 2, N], F32), ps("pO", [P, 2, 512], F32))


def program(nc, x, wqk, wv, woc, wqkv, wo, qk_scales, ln_g, ln_b, w1, b1, w2, b2, tables, out):
    with ExitStack() as c:
        sb = lambda n, s, d: c.enter_context(nc.sbuf_tensor(n, s, d))
        X = nc.dram_tensor("X", [(2 * LAYERS + 1) * ST_ROWS, D], F32, kind="Internal").ap()
        QKP = nc.dram_tensor("QKP", [BATCH * CG, P, 3, SEQ], BF16, kind="Internal").ap()
        VA = nc.dram_tensor("VA", [TOK, CH * VW], F32, kind="Internal").ap()
        AO = nc.dram_tensor("AO", [TOK, D], F32, kind="Internal").ap()

        K = Named()
        K.passed = c.enter_context(nc.semaphore("passed"))
        K.ident = sb("ident", [P, P], F32)
        K.identb = sb("identb", [P, P], BF16)
        K.mhalf = sb("mhalf", [P, 2 * LH], F32)
        K.zeros = sb("zeros", [(2 * LAYERS + 1) * BATCH, D], F32)
        K.masks = sb("masks", [P, 3, 4 * P], BF16)
        K.base = sb("base", [P, TPB, 4, LD], F32)
        WS = semaphores(c, nc, "w_", (
            "w_loaded", "w_hi", "w_split", "cleared", "tab_ready", "x1_ready", "ss_ready", "k_copied", "sq_ready",
            "added", "ts_ready", "ssc_ready", "rs_ready", "rsum_ready", "pn_ready", "t_ready", "t_hi", "t_lo",
            "q_ready", "k_ready", "v_ready", "q_copied", "v_copied", "max_ready", "exp_done", "pt_ready",
            "pt_even", "pt_odd", "kt_ready", "kt_copied", "qt_ready", "qt_copied", "ot_ready", "ot_hi", "ot_lo",
            "tc_ready", "qkn_ready", "s_ready", "wo_ready"), {"qkv_loaded": 3, "x_loaded": 4, "x1_stored": 2})
        FS = semaphores(c, nc, "f_", (
            "w_loaded", "w1_loaded", "ln_loaded", "w_hi", "w_split", "cleared", "x2_ready", "hn_ready", "xb_ready", "mv_ready", "ve_ready",
            "rstd_ready", "act_ready", "a_hi", "a_lo", "t_ready", "t_hi", "t_lo", "hf_ready", "g_ready",
            "gelu_done", "stats", "o_ready"), {"h_loaded": 2, "x_loaded": 2, "x2_stored": 2})
        K.starts = [(x, ONE) for sems in (WS, FS) for v in sems.values() for x in (v if isinstance(v, list) else [v])]
        K.starts += [(WS["kt_copied"], 1), (WS["exp_done"], 2), (WS["x1_ready"], 2), (WS["ot_lo"], 2),
                     (WS["qt_copied"], 1), (FS["act_ready"], 2), (FS["x2_ready"], 2), (FS["a_lo"], 1)]
        made = c.enter_context(nc.semaphore("made"))
        K.zeroed = zeroed = c.enter_context(nc.semaphore("zeroed"))
        with nc.Block() as block:
            @block.gpsimd
            def _(pool):
                pool.memset(K.mhalf[:, :], -0.5)
                pool.memset(K.zeros[:, :], 0.0).then_inc(made, 1)
                pool.wait_ge(made, 1)
                pool.memset(K.ident[:, :], 0.0).then_inc(made, 1)
                pool.memset(K.identb[:, :], 0.0).then_inc(made, 1)
                pool.wait_ge(made, 3)
                for t in (K.ident, K.identb):
                    pool.affine_select(out=t[:, :], in_=t[:, :], compare_op=ALU.not_equal, fill=1.0,
                                       base=0, pattern=[[-1, P]], channel_multiplier=1).then_inc(made, 1)

            @block.sync
            def _(sp):
                sp.dma_start(K.base[:, :, :, :], tables).then_inc(zeroed, 16)
                sp.wait_ge(made, 1)
                sp.dma_start(X.rearrange("(g r) d -> g r d", r=SEQ + 1)[:, 0, :], K.zeros[:, :]).then_inc(zeroed, 16)
        with ExitStack() as c1:
            K.stacks = (c1.enter_context(nc.sbuf_tensor("ca_qs", [SROWS, SLOTS, GH, SEQ], BF16)),
                        c1.enter_context(nc.sbuf_tensor("ca_ks", [SROWS, SLOTS, GH, SEQ], BF16)),
                        c1.enter_context(nc.sbuf_tensor("ca_va", [P, SLOTS, TPB, GH * VW], F32)),
                        [c1.enter_context(nc.semaphore(f"ca_loaded{i}")) for i in range(SLOTS)])
            phase_project(nc, K, x, X, QKP, VA, wqk, wv)
            phase_causal(nc, K, QKP, VA, AO)
        with ExitStack() as c2:
            sb2 = lambda n, s, d: c2.enter_context(nc.sbuf_tensor(n, s, d))
            weights = (sb2("big_st", [P, KD, 2 * HC * P], F32), sb2("big_hi", [P, KD, 2 * HC * P], F32R),
                       sb2("big_lo", [P, KD, 2 * HC * P], F32R))
            W, F = Named(), Named()
            W.weights, W.sems, F.sems = weights, WS, FS
            F.hh = sb2("f_hh", [P, 2, SUP, D], F32)
            with nc.Fori(0, LAYERS) as layer:
                with ExitStack() as cw:
                    window_tensors(nc, cw, W)
                    phase_window(nc, K, W, F, layer, X, wqkv, wo, qk_scales, w1)
                with ExitStack() as cf:
                    feed_tensors(nc, cf, F)
                    phase_feed(nc, K, W, F, layer, X, ln_g, ln_b, b1, w2, b2)
        phase_output(nc, K, AO, X, x, woc, out)


def rotary_tables():
    f = np.float32
    half = np.arange(0, LD, 2, dtype=f)
    inv = (f(1) / f(10000) ** (half / f(LD))).astype(f)
    t = np.arange(SEQ, dtype=f)
    freqs = t[:, None] * inv[None, :]
    base = ((half + f(0.4 * LD)) / f(1.4 * LD)).astype(f)
    scale = base[None, :] ** ((t - SEQ // 2) / f(P // 2))[:, None]
    cos, sin = np.cos(freqs), np.sin(freqs)
    two = lambda a, b: np.concatenate([a, b], axis=-1)
    out = np.stack([two(cos * scale, cos * scale) * f(QK_SCALE), two(-sin * scale, sin * scale) * f(QK_SCALE),
                    two(cos / scale, cos / scale), two(-sin / scale, sin / scale)], axis=1)
    return np.ascontiguousarray(out.reshape(TPB, P, 4, LD).transpose(1, 0, 2, 3).astype(f))


def kernel(**inputs):
    import concourse.bacc as bacc
    from concourse.bass_utils import run_bass_kernel_spmd

    g = {k: np.ascontiguousarray(v) for k, v in inputs.items()}
    wq, wk = (g[f"L0_attn_W_{n}"].T.reshape(D, CG, GH * CD) for n in "qk")
    scales = np.stack([h for n in "qk" for s in [g[f"L0_ffn_{n}_scale"]] for h in (s, np.roll(s, LD // 2, axis=-1))],
                      axis=1)
    arrays = {
        "x": g["L0_attn_x"].reshape(TOK, D),
        "wqk": np.ascontiguousarray(np.stack([wq, wk], axis=2).reshape(D, 2 * D)),
        "wv": np.ascontiguousarray(g["L0_attn_W_v"].T),
        "woc": np.ascontiguousarray(g["L0_attn_W_o"].T),
        "qk_scales": np.ascontiguousarray(scales),
        **{n: g["L0_ffn_" + n] for n in ("wqkv", "wo", "ln_g", "ln_b", "w1", "b1", "w2", "b2")},
        "tables": rotary_tables(),
    }
    nc = bacc.Bacc("TRN2", target_bir_lowering=False, num_devices=1)
    args = {n: nc.dram_tensor(n, a.shape, mybir.dt.from_np(a.dtype), kind="ExternalInput").ap()
            for n, a in arrays.items()}
    out = nc.dram_tensor("out", (TOK, D), F32, kind="ExternalOutput").ap()
    program(nc, out=out, **args)
    r = run_bass_kernel_spmd(nc, [arrays], core_ids=[0])
    return r.results[0]["out"].reshape(BATCH, SEQ, D)
```
